# Optimizing a Trainium2 kernel written in Bass

```python
import numpy as np
import jax
import jax.numpy as jnp

def _softmax(x, axis=-1):
    return jax.nn.softmax(x, axis=axis)

def _gelu(x):
    return jax.nn.gelu(x, approximate=True)

def _silu(x):
    return jax.nn.silu(x)

def _sigmoid(x):
    return jax.nn.sigmoid(x)

def _layernorm(x, axis=-1, eps=1e-05):
    m = jnp.mean(x, axis=axis, keepdims=True)
    v = jnp.var(x, axis=axis, keepdims=True)
    return (x - m) / jnp.sqrt(v + eps)

def _scatter_add(tgt, idx, src, axis=0):
    return tgt.at[idx].add(src)

def _segment_sum(src, seg, n):
    return jax.ops.segment_sum(src, seg, n)
kernel_name = 'mk_gnn_resnorm_d1_gnn_r64_60270e'

def setup_inputs(seed: int=0):
    np.random.seed(seed)
    _w = jnp.asarray

    def _rec_inputs():
        import jax
        import jax.numpy as jnp
        _gk = jax.random.key(seed)
        x = -0.000202 + 1 * jax.random.normal(jax.random.fold_in(_gk, 1), (50000, 128), jnp.float32)
        src = jax.random.randint(jax.random.fold_in(_gk, 2), (12500,), 0, 50000, jnp.int32)
        dst = jnp.minimum((50000 * jax.random.uniform(jax.random.fold_in(_gk, 3), (12500,)) ** 2.0).astype(jnp.int32), 49999)
        _o = jnp.argsort(dst, stable=True)
        src = src[_o]
        dst = dst[_o]
        edge_attr_128 = -5.16925e-05 + 1.00005 * jax.random.normal(jax.random.fold_in(_gk, 11), (12500, 128), jnp.float32)
        return (x, src, dst, edge_attr_128)
    x, src, dst, edge_attr_128 = _rec_inputs()

    def _L0_gnn_setup():
        import jax, jax.numpy as jnp
        import numpy as np
        N_NODES = 50000
        N_EDGES = 12500
        X_DIM = 128
        HID = 128
        IN_CH = X_DIM + HID
        OUT_CH = 128
        key = jax.random.key(seed)
        ks = jax.random.split(key, 10)
        x = jax.random.normal(ks[0], (N_NODES, X_DIM), dtype=jnp.float32)
        edge_index = jax.random.randint(ks[1], (2, N_EDGES), 0, N_NODES, dtype=jnp.int64)
        edge_attr = jax.random.normal(ks[2], (N_EDGES, HID), dtype=jnp.float32)

        def lin(k, fan_in, fan_out):
            k1, k2 = jax.random.split(k)
            bound = 1.0 / np.sqrt(fan_in)
            W = jax.random.uniform(k1, (fan_in, fan_out), minval=-bound, maxval=bound, dtype=jnp.float32)
            b = jax.random.uniform(k2, (fan_out,), minval=-bound, maxval=bound, dtype=jnp.float32)
            return (W, b)
        W0, b0 = lin(ks[3], IN_CH, HID)
        W2, b2 = lin(ks[4], HID, HID)
        W3, b3 = lin(ks[5], HID, OUT_CH)
        return {'x': x, 'edge_index': edge_index, 'edge_attr': edge_attr, 'W0': W0, 'b0': b0, 'W2': W2, 'b2': b2, 'W3': W3, 'b3': b3}
    _L0_gnn_all = _L0_gnn_setup()
    _L0_gnn_in = {k: v for k, v in _L0_gnn_all.items() if k in ('W0', 'b0', 'W2', 'b2', 'W3', 'b3')}
    del _L0_gnn_all
    return {'x': x, 'src': src, 'dst': dst, 'edge_attr_128': edge_attr_128, 'L0_gnn_W0': _L0_gnn_in['W0'], 'L0_gnn_b0': _L0_gnn_in['b0'], 'L0_gnn_W2': _L0_gnn_in['W2'], 'L0_gnn_b2': _L0_gnn_in['b2'], 'L0_gnn_W3': _L0_gnn_in['W3'], 'L0_gnn_b3': _L0_gnn_in['b3']}

def reference(x, src, dst, edge_attr_128, L0_gnn_W0, L0_gnn_b0, L0_gnn_W2, L0_gnn_b2, L0_gnn_W3, L0_gnn_b3):
    import jax
    import jax.numpy as jnp

    def _L0_gnn_ref(x, edge_index, edge_attr, W0, b0, W2, b2, W3, b3):
        import jax, jax.numpy as jnp
        import numpy as np
        N_NODES = 50000
        N_EDGES = 12500
        X_DIM = 128
        HID = 128
        IN_CH = X_DIM + HID
        OUT_CH = 128
        edge_sum = jax.ops.segment_sum(edge_attr, edge_index[0], num_segments=x.shape[0])
        inputs = jnp.concatenate([x, edge_sum], axis=1)
        h = jax.nn.elu(inputs @ W0 + b0)
        h = jax.nn.elu(h @ W2 + b2)
        out = h @ W3 + b3
        return out
    edge_index = jnp.stack([src, dst])
    x = _layernorm(x + _L0_gnn_ref(x, edge_index, edge_attr_128, L0_gnn_W0, L0_gnn_b0, L0_gnn_W2, L0_gnn_b2, L0_gnn_W3, L0_gnn_b3), axis=-1)
    return x

_drawn_inputs = setup_inputs


def setup_inputs(seed=0):
    import zlib

    import numpy as np

    out = dict(_drawn_inputs(seed))
    spreads = {}
    factors = {'L0_gnn_b0': 5.114}
    for name, (base, spread) in spreads.items():
        noise = np.random.default_rng([zlib.crc32(name.encode()), seed]).standard_normal(out[name].shape)
        drawn = base * np.exp(spread * noise) if base else spread * noise
        out[name] = jnp.asarray(drawn.astype(out[name].dtype))
    for name, factor in factors.items():
        out[name] = (out[name] * factor).astype(out[name].dtype)
    return out
```

```python
from contextlib import ExitStack

import concourse.bass as bass
from concourse import mybir

ALU = mybir.AluOpType
ACT = mybir.ActivationFunctionType
AX_X = mybir.AxisListType.X
F32 = mybir.dt.float32
BF16 = mybir.dt.bfloat16
I32 = mybir.dt.int32

P = 128
J = 4
EP = 125
DIG = 256
NPAY = 4
EPS = 1e-5
ROUND = 12582912.0
SKIP = 65536.0


def gnn_resnorm(nc, x, src, attr, W0, b0, W2, b2, W3, b3, key_rows, out):
    N, F = x.shape
    E = src.shape[0]
    assert F == P and E % (EP * J) == 0 and N < DIG * DIG and N < SKIP
    EC = E // EP
    ROWS = J * P
    COLS = J * EP
    ND = -(-N // ROWS)
    NE = EC // J
    NI = ND + NE
    SLOTS = 4

    with ExitStack() as ctx:
        def sb(name, shape, dt=F32):
            return ctx.enter_context(nc.sbuf_tensor(name, shape, dt))

        def psum(name, shape):
            return ctx.enter_context(nc.psum_tensor(name, shape, F32))

        def sem(name):
            return ctx.enter_context(nc.semaphore(name))

        xT_ps = psum("xT_ps", [P, 2, J * P])
        l1_ps = psum("l1_ps", [P, J * P])
        l2_ps = psum("l2_ps", [P, J * P])
        z_ps = psum("z_ps", [P, 2, J * P])
        rank_ps = psum("rank_ps", [P, J * P])
        perm_ps = psum("perm_ps", [P, J * P])

        w0x = sb("w0x", [P, P])
        w0e = sb("w0e", [P, P])
        w2 = sb("w2", [P, P])
        w3 = sb("w3", [P, P])
        w3c = sb("w3c", [P, P])
        b_in = sb("b_in", [P, 3])
        w3_sum = sb("w3_sum", [P, 1])
        w3_mean = sb("w3_mean", [P, 1])
        minus_one = sb("minus_one", [P, 1])
        bias_x = sb("bias_x", [P, 1])
        bias1 = sb("bias1", [P, 1])
        neg_bias1 = sb("neg_bias1", [P, 1])
        bias2 = sb("bias2", [P, 1])
        neg_bias2 = sb("neg_bias2", [P, 1])
        neg_half = sb("neg_half", [P, J])

        diff_i = sb("diff_i", [P, P], I32)
        diff = sb("diff", [P, P])
        count_i = sb("count_i", [P, DIG], I32)
        count = sb("count", [P, DIG], BF16)
        prow_i = sb("prow_i", [P, 1], I32)
        ident = sb("ident", [P, P])
        center = sb("center", [P, P])
        before = sb("before", [P, P], BF16)
        not_before = sb("not_before", [P, P], BF16)
        ones = sb("ones", [P, P], BF16)
        next_row = sb("next_row", [P, P])
        next_col = sb("next_col", [P, P])

        src_i = sb("src_i", [P, EC], I32)
        digit_i = sb("digit_i", [P, 2, EC], I32)
        pay = sb("pay", [P, NPAY, EC + J])
        onehot = sb("onehot", [P, 4, DIG], BF16)
        totals = sb("totals", [P, DIG])
        zeros = sb("zeros", [P, DIG])
        zeros_b = sb("zeros_b", [P, J * P], BF16)
        start = sb("start", [P, DIG])
        start_i = sb("start_i", [P, 3, DIG], I32)
        start_b = sb("start_b", [P, 2, DIG], BF16)
        picked = sb("picked", [P, 2, DIG])
        pos = sb("pos", [P, EC])
        quot = sb("quot", [P, EC])
        pos_col = sb("pos_col", [P, EC])
        pos_row = sb("pos_row", [P, EC])
        row_hot = sb("row_hot", [P, 4, EP], BF16)
        col_pay = sb("col_pay", [P, 4, NPAY, EC], BF16)

        key = sb("key", [P, EC + 1])
        key_i = sb("key_i", [P, EC], I32)
        edge_f = sb("edge_f", [P, EC])
        edge_i = sb("edge_i", [P, EC], I32)
        dup = sb("dup", [P, EC])
        target = sb("target", [P, EC])
        target_i = sb("target_i", [P, EC], I32)
        keyT = sb("keyT", [P, EP])
        keyB = sb("keyB", [P, E])
        attr_sb = sb("attr_sb", [P, 2, J, P])
        same = sb("same", [P, 4, EP])
        sumT = sb("sumT", [P, E])
        lastT = sb("lastT", [P, EC])
        last_w = sb("last_w", [P, P])
        carry = sb("carry", [P, 2, COLS])
        attr_idx = sb("attr_idx", [P, 2, J], I32)
        x_idx = sb("x_idx", [P, SLOTS, J], I32)
        out_idx = sb("out_idx", [P, SLOTS, J], I32)

        x_sb = sb("x_sb", [P, SLOTS, J * P])
        xT = sb("xT", [P, SLOTS, J * P])
        e1 = sb("e1", [P, 2, J * P])
        e2 = sb("e2", [P, 2, J * P])
        h1 = sb("h1", [P, 2, J * P])
        h2 = sb("h2", [P, 2, J * P])
        sq = sb("sq", [P, 2, J * P])
        ssq = sb("ssq", [P, 2, J])
        var_eps = sb("var_eps", [P, 2, J])
        rstd = sb("rstd", [P, 2, J])
        o_sb = sb("o_sb", [P, SLOTS, J * P])

        weights_loaded = sem("weights_loaded")
        src_loaded = sem("src_loaded")
        consts_made = sem("consts_made")
        dve_chain = sem("dve_chain")
        pool_waits = sem("pool_waits")
        setup_mm = sem("setup_mm")
        b3_ready = sem("b3_ready")
        biases_ready = sem("biases_ready")
        onehot_ready = sem("onehot_ready")
        onehot_used = sem("onehot_used")
        hist_done = sem("hist_done")
        start_ready = sem("start_ready")
        rank_ready = sem("rank_ready")
        rank_read = sem("rank_read")
        place_ready = sem("place_ready")
        place_used = sem("place_used")
        permuted = sem("permuted")
        key_ready = sem("key_ready")
        key_mm = sem("key_mm")
        keyT_ready = sem("keyT_ready")
        keys_stored = sem("keys_stored")
        keyB_loaded = sem("keyB_loaded")
        index_ready = sem("index_ready")
        attr_idx_ready = sem("attr_idx_ready")
        attr_loaded = [sem(f"attr_loaded{k}") for k in range(2)]
        same_ready = sem("same_ready")
        same_used = sem("same_used")
        sum_ps_ready = sem("sum_ps_ready")
        sum_ready = sem("sum_ready")
        last_ready = sem("last_ready")
        last_mm = sem("last_mm")
        last_w_ready = sem("last_w_ready")
        carry_ready = sem("carry_ready")

        x_loaded = [sem(f"x_loaded{k}") for k in range(SLOTS)]
        xg_loaded = [sem(f"xg_loaded{k}") for k in range(SLOTS)]
        x_idx_ready = sem("x_idx_ready")
        out_idx_ready = sem("out_idx_ready")
        xT_ps_ready = sem("xT_ps_ready")
        xT_ready = sem("xT_ready")
        l1_ready = sem("l1_ready")
        exp1_ready = sem("exp1_ready")
        min1_ready = sem("min1_ready")
        h1_ready = sem("h1_ready")
        l2_ready = sem("l2_ready")
        exp2_ready = sem("exp2_ready")
        min2_ready = sem("min2_ready")
        h2_ready = sem("h2_ready")
        z_ready = sem("z_ready")
        sq_ready = sem("sq_ready")
        ssq_ready = sem("ssq_ready")
        var_ready = sem("var_ready")
        rstd_ready = sem("rstd_ready")
        o_ready = sem("o_ready")
        stored = [sem(f"stored{k}") for k in range(SLOTS)]
        scattered = [sem(f"scattered{k}") for k in range(SLOTS)]

        DENSE_ON = [len(range(k, ND, SLOTS)) for k in range(SLOTS)]

        def at_least(eng, semaphore, const, reg=0):
            if isinstance(reg, int):
                if const + reg > 0:
                    eng.wait_ge(semaphore, const + reg)
            else:
                eng.wait_ge(semaphore, reg + const)

        def pool_at_least(pool, semaphore, const, reg=0):
            if isinstance(reg, int):
                at_least(pool, semaphore, const, reg)
                return
            pool.wait_ge(semaphore, reg + const)
            pool.sem_inc(pool_waits, 1)

        def is_edge(c):
            return c >= ND

        def item_in(c, edge_loop=None):
            return 0 <= c < NI

        def slot_count(c, m):
            return (c - ND) // SLOTS, m

        STEPS_END = NI + 4
        HEAD = 8
        LOOP1 = (ND - HEAD) // 4
        MID = HEAD + 4 * LOOP1
        LOOP2_AT = -(-(ND + 4) // 4) * 4
        LOOP2 = (NI - LOOP2_AT) // 4

        def walk(eng, step, at_mid=None):
            for c in range(HEAD):
                step(c, 0, 0)
            with eng.Fori(0, LOOP1) as m:
                for u in range(4):
                    step(HEAD + u, m * 4, m)
            if at_mid is not None:
                at_mid()
            for c in range(MID, LOOP2_AT):
                step(c, 0, 0)
            with eng.Fori(0, LOOP2) as m:
                for u in range(4):
                    step(LOOP2_AT + u, m * 4, m)
            for c in range(LOOP2_AT + 4 * LOOP2, STEPS_END):
                step(c, 0, 0)

        def cols(c):
            return COLS if is_edge(c) else ROWS

        block = ctx.enter_context(nc.Block())

        @block.sync
        def _(sp):
            sp.dma_start(src_i[0:EP, :], src.rearrange("(p c) -> p c", p=EP)).then_inc(src_loaded, 16)
            sp.dma_start(w0x[:], W0[0:P, :]).then_inc(weights_loaded, 16)
            sp.dma_start(w0e[:], W0[P:2 * P, :]).then_inc(weights_loaded, 16)
            sp.dma_start(w2[:], W2[:, :]).then_inc(weights_loaded, 16)
            sp.dma_start(w3[:], W3[:, :]).then_inc(weights_loaded, 16)
            for k, b in enumerate((b0, b2, b3)):
                sp.dma_start(b_in[:, k:k + 1], b.rearrange("(p a) -> p a", a=1)).then_inc(weights_loaded, 16)

            def key_round_trip():
                sp.wait_ge(keyT_ready, 1)
                sp.dma_start(key_rows.rearrange("(c e) -> c e", e=EP), keyT[0:EC, :]).then_inc(keys_stored, 16)
                sp.wait_ge(keys_stored, 16)
                sp.dma_start(keyB[:], key_rows.rearrange("(a e) -> a e", a=1).to_broadcast([P, E])).then_inc(keyB_loaded, 16)

            key_round_trip()

            def rows_of(ap, c, m):
                if c == ND - 1:
                    part = ap[N - ROWS:N, :]
                elif isinstance(m, int):
                    part = ap[c * ROWS:(c + 1) * ROWS, :]
                else:
                    part = ap[bass.ds(m * (4 * ROWS) + c * ROWS, ROWS), :]
                return part.rearrange("(p j) f -> p (j f)", p=P)

            def step(c, m4, m):
                if c < ND:
                    at_least(sp, xT_ps_ready, c - SLOTS + 1, m4)
                    sp.dma_start(x_sb[:, c % SLOTS, :], rows_of(x, c, m)).then_inc(x_loaded[c % SLOTS], 16)
                i = c - 4
                if 0 <= i < ND:
                    at_least(sp, o_ready, i + 1, m4)
                    if i == ND - 1:
                        sp.wait_ge(stored[(i - 1) % SLOTS], 16 * DENSE_ON[(i - 1) % SLOTS])
                    sp.dma_start(rows_of(out, i, m), o_sb[:, i % SLOTS, :]).then_inc(stored[i % SLOTS], 16)

            for c in range(HEAD):
                step(c, 0, 0)
            with sp.Fori(0, LOOP1) as m:
                for u in range(4):
                    step(HEAD + u, m * 4, m)
            for c in range(MID, ND + 4):
                step(c, 0, 0)
            for k in range(SLOTS):
                sp.wait_ge(stored[k], 16 * DENSE_ON[k])

        @block.gpsimd
        def _(pool):
            nc.gpsimd.iota(diff_i[:], pattern=[[1, P]], base=0, channel_multiplier=-1).then_inc(consts_made, 1)
            nc.gpsimd.iota(count_i[:], pattern=[[1, DIG]], base=0, channel_multiplier=0).then_inc(consts_made, 1)
            nc.gpsimd.iota(prow_i[:], pattern=[[0, 1]], base=0, channel_multiplier=1).then_inc(consts_made, 1)

            def gather_attr(g, r, gp):
                pool_at_least(pool, attr_loaded[gp], 64 * (g // 2), r if isinstance(r, int) else r * 32)
                pool_at_least(pool, same_used, J * (g - 1), r if isinstance(r, int) else r * J)
                a = J * g if isinstance(r, int) else r * J + J * g
                nc.gpsimd.tensor_copy(attr_idx[0:EP, gp, :], edge_i[0:EP, bass.ds(a, J)]).then_inc(attr_idx_ready, 1)
                pool_at_least(pool, attr_idx_ready, g + 1, r)
                for j in range(J):
                    nc.gpsimd.indirect_dma_start(
                        out=attr_sb[0:EP, gp, j, :], out_offset=None, in_=attr[:, :],
                        in_offset=bass.IndirectOffsetOnAxis(ap=attr_idx[0:EP, gp, j:j + 1], axis=0),
                    ).then_inc(attr_loaded[gp], 16)

            def prepass():
                pool.wait_ge(index_ready, 1)
                for g in range(3):
                    gather_attr(g, 0, g % 2)
                with pool.Fori(0, (NE - 3) // 2) as h:
                    gather_attr(3, h * 2, 1)
                    gather_attr(4, h * 2, 0)

            def gather_x(c, m4, m):
                k = c % SLOTS
                before_, r = slot_count(c, m)
                pool_at_least(pool, xg_loaded[k], 64 * before_, r * 64)
                pool_at_least(pool, xT_ps_ready, c - SLOTS + 1, m4)
                a = (c - ND) * J if isinstance(m, int) else m4 * J + (c - ND) * J
                nc.gpsimd.tensor_copy(x_idx[0:EP, k, :], key_i[0:EP, bass.ds(a, J)]).then_inc(x_idx_ready, 1)
                pool_at_least(pool, x_idx_ready, c - ND + 1, m4)
                for j in range(J):
                    nc.gpsimd.indirect_dma_start(
                        out=x_sb[0:EP, k, j * P:(j + 1) * P], out_offset=None, in_=x[:, :],
                        in_offset=bass.IndirectOffsetOnAxis(ap=x_idx[0:EP, k, j:j + 1], axis=0),
                    ).then_inc(xg_loaded[k], 16)

            def scatter_out(c, m4, m):
                k = c % SLOTS
                before_, r = slot_count(c, m)
                pool_at_least(pool, scattered[k], 64 * before_, r * 64)
                pool_at_least(pool, o_ready, c + 1, m4)
                a = (c - ND) * J if isinstance(m, int) else m4 * J + (c - ND) * J
                nc.gpsimd.tensor_copy(out_idx[0:EP, k, :], target_i[0:EP, bass.ds(a, J)]).then_inc(out_idx_ready, 1)
                pool_at_least(pool, out_idx_ready, c - ND + 1, m4)
                for j in range(J):
                    nc.gpsimd.indirect_dma_start(
                        out=out[:, :], out_offset=bass.IndirectOffsetOnAxis(ap=out_idx[0:EP, k, j:j + 1], axis=0),
                        in_=o_sb[0:EP, k, j * P:(j + 1) * P], in_offset=None,
                        bounds_check=N - 1, oob_is_err=False,
                    ).then_inc(scattered[k], 16)

            def clamp(c, m4, exp_sb, exp_ready, bias, done):
                pool_at_least(pool, exp_ready, c + 1, m4)
                v = exp_sb[:, c % 2, 0:cols(c)]
                nc.gpsimd.tensor_scalar(v, v, 1.0, bias[:, 0:1], ALU.min, ALU.add).then_inc(done, 1)

            def step(c, m4, m):
                if is_edge(c) and c < NI:
                    gather_x(c, m4, m)
                if item_in(c - 1):
                    clamp(c - 1, m4, e1, exp1_ready, bias1, min1_ready)
                if item_in(c - 2):
                    clamp(c - 2, m4, e2, exp2_ready, bias2, min2_ready)
                if item_in(c - 3):
                    i = c - 3
                    q = slice(0, EP if is_edge(i) else P)
                    pool_at_least(pool, ssq_ready, i + 1, m4)
                    nc.gpsimd.tensor_scalar(var_eps[q, i % 2, :], ssq[q, i % 2, :], EPS, None, ALU.add).then_inc(var_ready, 1)
                    pool_at_least(pool, var_ready, i + 1, m4)
                    pool_at_least(pool, o_ready, i - 1, m4)
                    nc.gpsimd.tensor_tensor(rstd[q, i % 2, :], var_eps[q, i % 2, :], neg_half[q, :], ALU.pow).then_inc(rstd_ready, 1)
                if item_in(c - 4) and is_edge(c - 4):
                    scatter_out(c - 4, m4, m)

            def mid():
                prepass()

            for c in range(HEAD):
                if c == 0:
                    pool.wait_ge(biases_ready, 1)
                step(c, 0, 0)
            with pool.Fori(0, LOOP1) as m:
                for u in range(4):
                    step(HEAD + u, m * 4, m)
            mid()
            for c in range(MID, LOOP2_AT):
                if c == ND + 4:
                    for k in range(SLOTS):
                        pool.wait_ge(stored[k], 16 * DENSE_ON[k])
                step(c, 0, 0)
            assert LOOP2_AT <= ND + 4 + 3
            if LOOP2_AT <= ND + 4:
                for k in range(SLOTS):
                    pool.wait_ge(stored[k], 16 * DENSE_ON[k])
            with pool.Fori(0, LOOP2) as m:
                for u in range(4):
                    step(LOOP2_AT + u, m * 4, m)
            for c in range(LOOP2_AT + 4 * LOOP2, STEPS_END):
                step(c, 0, 0)
            for k in range(SLOTS):
                pool.wait_ge(scattered[k], 64 * len([i for i in range(ND, NI) if i % SLOTS == k]))

        @block.tensor
        def _(pe):
            def small_products():
                pe.wait_ge(weights_loaded, 16 * 7)
                pe.wait_ge(b3_ready, 1)
                nc.tensor.matmul(l1_ps[:, 0:1], w2[:], minus_one[:], start=True, stop=True)
                nc.tensor.matmul(l2_ps[:, 0:1], center[:], b_in[:, 2:3], start=True, stop=False)
                nc.tensor.matmul(l2_ps[:, 0:1], w3c[:], minus_one[:], start=False, stop=True).then_inc(setup_mm, 1)
                pe.wait_ge(b3_ready, 2)
                nc.tensor.matmul(z_ps[:, 0, 0:1], w0x[:], bias_x[:], start=True, stop=True).then_inc(setup_mm, 1)

            def hot(c):
                return onehot[0:EP, c % 4, :]

            def sort_pass(n):
                done = n * EC
                def hist(c, r):
                    at_least(pe, onehot_ready, 2 * n * (EC + 1) - n + c + 1, r)
                    nc.tensor.matmul(perm_ps[0:EP, 0:DIG], ones[0:EP, 0:EP], hot(c), start=False, stop=False,
                                     skip_group_check=True).then_inc(onehot_used, 1)
                zero = zeros_b[0:EP, :]
                pe.wait_ge(start_ready, 1 + 2 * n)
                nc.tensor.matmul(perm_ps[0:EP, :], ones[0:EP, 0:EP], zero, start=True, stop=False, skip_group_check=True)
                with pe.Fori(0, EC // 4) as m:
                    for u in range(4):
                        hist(u, m * 4)
                nc.tensor.matmul(perm_ps[0:EP, :], ones[0:EP, 0:EP], zero, start=False, stop=True,
                                 skip_group_check=True).then_inc(hist_done, 1)
                pe.wait_ge(start_ready, 2 + 2 * n)
                for bank in (rank_ps, perm_ps):
                    for part in range(2):
                        nc.tensor.matmul(bank[0:EP, 0:DIG], ones[0:1, 0:EP], start_b[0:1, part, :],
                                         start=(part == 0), stop=False, skip_group_check=True)

                def rank(c, r):
                    bank = (rank_ps, perm_ps)[c % 2][0:EP, 0:DIG]
                    at_least(pe, onehot_ready, 2 * n * (EC + 1) - n + EC + c + 1, r)
                    if n > 0 or c > 1 or not isinstance(r, int):
                        at_least(pe, rank_read, n * EC + c - 1, r)
                    nc.tensor.matmul(bank, not_before[0:EP, 0:EP], hot(c + 2), start=False, stop=False, skip_group_check=True)
                    nc.tensor.matmul(bank, ones[0:EP, 0:EP], hot(c + 3), start=False, stop=False, skip_group_check=True)
                    nc.tensor.matmul(bank, before[0:EP, 0:EP], hot(c), start=False, stop=False,
                                     skip_group_check=True).then_inc(rank_ready, 1)
                for c in range(4):
                    rank(c, 0)
                with pe.Fori(0, EC // 4 - 1) as m:
                    for u in range(4):
                        rank(4 + u, m * 4)
                pe.wait_ge(rank_read, (n + 1) * EC)

                def permute(c, r):
                    at_least(pe, place_ready, n * EC + c + 1, r)
                    nc.tensor.matmul(perm_ps[0:EP, 0:NPAY * EC], row_hot[0:EP, c % 4, :],
                                     col_pay[0:EP, c % 4, :, :].rearrange("p k c -> p (k c)"),
                                     start=False, stop=False, skip_group_check=True).then_inc(place_used, 1)
                nc.tensor.matmul(perm_ps[0:EP, :], ones[0:EP, 0:EP], zero, start=True, stop=False, skip_group_check=True)
                with pe.Fori(0, EC // 4) as m:
                    for u in range(4):
                        permute(u, m * 4)
                nc.tensor.matmul(perm_ps[0:EP, :], ones[0:EP, 0:EP], zero, start=False, stop=True,
                                 skip_group_check=True).then_inc(permuted, 1)

            def key_products():
                pe.wait_ge(key_ready, 1)
                nc.tensor.matmul(rank_ps[0:EP, 0:EC], next_row[0:EP, 0:EP], key[0:EP, 0:EC], start=True, stop=False)
                nc.tensor.matmul(rank_ps[0:EP, 0:EC], next_col[0:EP, 0:EP], key[0:EP, 1:EC + 1],
                                 start=False, stop=True).then_inc(key_mm, 1)
                nc.tensor.transpose(perm_ps[0:EC, 0:EP], key[0:EP, 0:EC], ident[0:EP, 0:EP]).then_inc(key_mm, 1)

            def sums_of(g, r, gp):
                ps = (rank_ps, perm_ps)[gp]
                at_least(pe, attr_loaded[gp], 64 * (g // 2 + 1), r if isinstance(r, int) else r * 32)
                at_least(pe, sum_ready, g - 1, r)
                for j in range(J):
                    at_least(pe, same_ready, J * g + j + 1, r if isinstance(r, int) else r * J)
                    mm = nc.tensor.matmul(ps[:, j * EP:(j + 1) * EP], attr_sb[0:EP, gp, j, :], same[0:EP, j, :],
                                          start=(j == 0), stop=(j == J - 1), skip_group_check=True)
                    mm.then_inc(same_used, 1)

            def prepass():
                pe.wait_ge(index_ready, 1)
                for g in range(3):
                    sums_of(g, 0, g % 2)
                with pe.Fori(0, (NE - 3) // 2) as h:
                    sums_of(3, h * 2, 1)
                    sums_of(4, h * 2, 0)
                pe.wait_ge(last_ready, 1)
                nc.tensor.matmul(perm_ps[0:EC, 0:P], lastT[:], w0e[:], start=True, stop=True).then_inc(last_mm, 1)

            def layer1(c, m4, m):
                i, n = c, cols(c)
                at_least(pe, xT_ready, i + 1, m4)
                at_least(pe, h1_ready, i, m4)
                ps = l1_ps[:, 0:n]
                if not is_edge(i):
                    nc.tensor.matmul(ps, w0x[:], xT[:, i % SLOTS, 0:n], start=True, stop=True).then_inc(l1_ready, 1)
                    return
                nc.tensor.matmul(ps, w0x[:], xT[:, i % SLOTS, 0:n], start=True, stop=False)
                a = (i - ND) * COLS if isinstance(m, int) else m * (4 * COLS) + (i - ND) * COLS
                nc.tensor.matmul(ps, w0e[:], sumT[:, bass.ds(a, COLS)], start=False, stop=False)
                at_least(pe, carry_ready, i - ND + 1, m4)
                nc.tensor.matmul(ps, last_w[0:EC, :], carry[0:EC, i % 2, :], start=False, stop=True).then_inc(l1_ready, 1)

            def turn(c, m4, m):
                if is_edge(c):
                    before_, r = slot_count(c, m)
                    at_least(pe, xg_loaded[c % SLOTS], 64 * (before_ + 1), r * 64)
                    q = EP
                else:
                    at_least(pe, x_loaded[c % SLOTS], 16 * (c // SLOTS + 1), m * 16)
                    q = P
                at_least(pe, xT_ready, c - 1, m4)
                for j in range(J):
                    mm = nc.tensor.transpose(xT_ps[:, c % 2, j * q:(j + 1) * q], x_sb[0:q, c % SLOTS, j * P:(j + 1) * P],
                                             ident[0:q, 0:q])
                mm.then_inc(xT_ps_ready, 1)

            def layer2(c, m4):
                n = cols(c)
                at_least(pe, h1_ready, c + 1, m4)
                at_least(pe, h2_ready, c, m4)
                nc.tensor.matmul(l2_ps[:, 0:n], w2[:], h1[:, c % 2, 0:n], start=True, stop=True).then_inc(l2_ready, 1)

            def layer3(c, m4):
                q = EP if is_edge(c) else P
                at_least(pe, h2_ready, c + 1, m4)
                at_least(pe, o_ready, c - 1, m4)
                for j in range(J):
                    z = z_ps[0:q, c % 2, j * P:(j + 1) * P]
                    nc.tensor.matmul(z, xT[:, c % SLOTS, j * q:(j + 1) * q], center[:], start=True, stop=False)
                    mm = nc.tensor.matmul(z, h2[:, c % 2, j * q:(j + 1) * q], w3c[:], start=False, stop=True)
                mm.then_inc(z_ready, 1)

            def step(c, m4, m):
                if item_in(c - 1):
                    layer1(c - 1, m4, m)
                if item_in(c):
                    turn(c, m4, m)
                if item_in(c - 2):
                    layer2(c - 2, m4)
                if item_in(c - 3):
                    layer3(c - 3, m4)

            small_products()
            sort_pass(0)
            sort_pass(1)
            key_products()
            pe.wait_ge(biases_ready, 1)
            walk(pe, step, at_mid=prepass)

        @block.scalar
        def _(act):
            def step(c, m4, m):
                if item_in(c):
                    n = cols(c)
                    at_least(act, xT_ps_ready, c + 1, m4)
                    at_least(act, z_ready, c - SLOTS + 1, m4)
                    nc.scalar.activation(xT[:, c % SLOTS, 0:n], xT_ps[:, c % 2, 0:n], ACT.Identity,
                                         bias=bias_x[:, 0:1]).then_inc(xT_ready, 1)
                if item_in(c - 1):
                    i = c - 1
                    n = cols(i)
                    at_least(act, l1_ready, i + 1, m4)
                    at_least(act, h1_ready, i - 1, m4)
                    nc.scalar.activation(e1[:, i % 2, 0:n], l1_ps[:, 0:n], ACT.Exp, bias=bias1[:, 0:1]).then_inc(exp1_ready, 1)
                if item_in(c - 2):
                    i = c - 2
                    n = cols(i)
                    at_least(act, l2_ready, i + 1, m4)
                    at_least(act, h2_ready, i - 1, m4)
                    nc.scalar.activation(e2[:, i % 2, 0:n], l2_ps[:, 0:n], ACT.Exp, bias=bias2[:, 0:1]).then_inc(exp2_ready, 1)
                if item_in(c - 3):
                    i = c - 3
                    q = EP if is_edge(i) else P
                    at_least(act, z_ready, i + 1, m4)
                    at_least(act, ssq_ready, i - 1, m4)
                    nc.scalar.activation(sq[0:q, i % 2, :], z_ps[0:q, i % 2, :], ACT.Square,
                                         scale=float(P) ** -0.5).then_inc(sq_ready, 1)

            act.wait_ge(biases_ready, 1)
            walk(act, step)

        @block.vector
        def _(dve):
            chain = [0]

            def link(ins):
                chain[0] += 1
                ins.then_inc(dve_chain, 1)
                dve.wait_ge(dve_chain, chain[0])

            V = nc.vector

            def constants():
                dve.wait_ge(consts_made, 3)
                V.memset(zeros[:], 0.0)
                V.memset(minus_one[:], -1.0)
                V.memset(neg_half[:], -0.5)
                V.memset(ones[:], 1.0)
                V.memset(pay[:], 0.0)
                V.memset(zeros_b[:], 0.0)
                V.memset(key[:], -1.0)
                V.tensor_copy(diff[:], diff_i[:])
                link(V.tensor_copy(count[:], count_i[:]))
                V.tensor_scalar(before[:], diff[:], 0.0, None, ALU.is_gt)
                V.tensor_scalar(not_before[:], diff[:], 0.0, None, ALU.is_le)
                V.tensor_scalar(next_row[:], diff[:], -1.0, None, ALU.is_equal)
                V.tensor_scalar(next_col[:], diff[:], float(EP - 1), None, ALU.is_equal)
                V.tensor_scalar(ident[:], diff[:], 0.0, None, ALU.is_equal)
                V.tensor_scalar(center[:], diff[:], 0.0, -1.0 / P, ALU.is_equal, ALU.add)
                V.tensor_copy(pay[0:EP, 2, 0:EC], prow_i[0:EP, 0:1].to_broadcast([EP, EC]))
                link(V.tensor_copy(pay[0:EP, 3, 0:EC], count_i[0:EP, 0:EC]))

            def biases():
                dve.wait_ge(weights_loaded, 16 * 7)
                link(V.reduce_sum(w3_sum[:], w3[:], AX_X))
                link(V.tensor_scalar(w3_mean[:], w3_sum[:], 1.0 / P, None, ALU.mult))
                V.tensor_scalar(w3c[:], w3[:], w3_mean[:, 0:1], None, ALU.subtract).then_inc(b3_ready, 1)
                dve.wait_ge(setup_mm, 1)
                V.tensor_scalar(bias2[:], l1_ps[:, 0:1], b_in[:, 1:2], None, ALU.add).then_inc(dve_chain, 1)
                V.tensor_copy(bias_x[:], l2_ps[:, 0:1]).then_inc(b3_ready, 1)
                chain[0] += 1
                dve.wait_ge(dve_chain, chain[0])
                V.tensor_scalar(neg_bias2[:], bias2[:], -1.0, None, ALU.mult)
                dve.wait_ge(setup_mm, 2)
                link(V.tensor_tensor(bias1[:], b_in[:, 0:1], z_ps[:, 0, 0:1], ALU.subtract))
                link(V.tensor_scalar(neg_bias1[:], bias1[:], -1.0, None, ALU.mult))
                V.memset(picked[:], 0.0).then_inc(biases_ready, 1)

            def digits():
                dve.wait_ge(src_loaded, 16)
                V.tensor_scalar(digit_i[0:EP, 0, :], src_i[0:EP, :], 8, None, ALU.logical_shift_right)
                link(V.tensor_scalar(digit_i[0:EP, 1, :], src_i[0:EP, :], DIG - 1, None, ALU.bitwise_and))
                link(V.tensor_copy(pay[0:EP, 0:2, 0:EC], digit_i[0:EP, :, :]))

            def sort_pass(n):
                d = 1 - n
                V.memset(zeros_b[0:1, 0:1], 0.0).then_inc(start_ready, 1)

                def make_onehot(c, r):
                    a = c if isinstance(r, int) else r + c
                    V.tensor_scalar(onehot[0:EP, c % 4, :], count[0:EP, :], pay[0:EP, d, bass.ds(a, 1)], None,
                                    ALU.is_equal).then_inc(onehot_ready, 1)

                def hist(c, r):
                    at_least(dve, onehot_used, n * EC + c - 3, r)
                    make_onehot(c, r)
                for c in range(4):
                    hist(c, 0)
                with dve.Fori(0, EC // 4 - 1) as m:
                    for u in range(4):
                        hist(4 + u, m * 4)
                dve.wait_ge(hist_done, n + 1)
                tot = perm_ps[0:EP, 0:DIG]
                link(V.tensor_tensor_scan(totals[0:EP, :], tot, zeros[0:EP, :], 0.0, ALU.add, ALU.add))
                link(V.tensor_tensor(start[0:EP, :], totals[0:EP, :], tot, ALU.subtract))
                link(V.tensor_copy(start_i[0:EP, 0, :], start[0:EP, :]))
                V.tensor_scalar(start_i[0:EP, 1, :], start_i[0:EP, 0, :], 127, None, ALU.bitwise_and)
                V.tensor_scalar(start_i[0:EP, 2, :], start_i[0:EP, 0, :], 65536 - 128, None, ALU.bitwise_and)
                link(V.memset(onehot[:, 2:4, :], 0.0))
                for part in range(2):
                    t = V.tensor_copy(start_b[0:EP, part, :], start_i[0:EP, 1 + part, :])
                t.then_inc(start_ready, 1)
                make_onehot(0, 0)

                def rank(c, r):
                    at_least(dve, rank_ready, n * EC + c, r)
                    make_onehot(c + 1, r)
                    at_least(dve, rank_ready, n * EC + c + 1, r)
                    a = c if isinstance(r, int) else r + c
                    V.scalar_tensor_tensor(out=picked[0:EP, c % 2, :], in0=(rank_ps, perm_ps)[c % 2][0:EP, 0:DIG], scalar=0.0,
                                           in1=onehot[0:EP, c % 4, :], op0=ALU.add, op1=ALU.mult,
                                           accum_out=pos[0:EP, bass.ds(a, 1)]).then_inc(rank_read, 1)
                for c in range(4):
                    rank(c, 0)
                with dve.Fori(0, EC // 4 - 1) as m:
                    for u in range(4):
                        rank(4 + u, m * 4)
                dve.wait_ge(rank_read, (n + 1) * EC)
                link(V.tensor_scalar(quot[0:EP, :], pos[0:EP, :], 1.0 / EP, -(EP // 2) / EP, ALU.mult, ALU.add))
                link(V.tensor_scalar(quot[0:EP, :], quot[0:EP, :], ROUND, None, ALU.add))
                link(V.tensor_scalar(pos_col[0:EP, :], quot[0:EP, :], ROUND, None, ALU.subtract))
                link(V.scalar_tensor_tensor(out=pos_row[0:EP, :], in0=pos_col[0:EP, :], scalar=-float(EP),
                                            in1=pos[0:EP, :], op0=ALU.mult, op1=ALU.add))

                def place(c, r):
                    a = c if isinstance(r, int) else r + c
                    at_least(dve, place_used, n * EC + c - 3, r)
                    V.tensor_scalar(row_hot[0:EP, c % 4, :], count[0:EP, 0:EP], pos_row[0:EP, bass.ds(a, 1)], None, ALU.is_equal)
                    for k in range(NPAY):
                        t = V.tensor_scalar(col_pay[0:EP, c % 4, k, :], count[0:EP, 0:EC], pos_col[0:EP, bass.ds(a, 1)],
                                            pay[0:EP, k, bass.ds(a, 1)], ALU.is_equal, ALU.mult)
                    t.then_inc(place_ready, 1)
                for c in range(4):
                    place(c, 0)
                with dve.Fori(0, EC // 4 - 1) as m:
                    for u in range(4):
                        place(4 + u, m * 4)
                dve.wait_ge(permuted, n + 1)
                link(V.tensor_copy(pay[0:EP, :, 0:EC], perm_ps[0:EP, 0:NPAY * EC].rearrange("p (k c) -> p k c", k=NPAY)))

            def keys():
                V.scalar_tensor_tensor(out=edge_f[0:EP, :], in0=pay[0:EP, 2, 0:EC], scalar=float(EC),
                                       in1=pay[0:EP, 3, 0:EC], op0=ALU.mult, op1=ALU.add)
                t = V.scalar_tensor_tensor(out=key[0:EP, 0:EC], in0=pay[0:EP, 0, 0:EC], scalar=float(DIG),
                                           in1=pay[0:EP, 1, 0:EC], op0=ALU.mult, op1=ALU.add)
                t.then_inc(key_ready, 1)
                dve.wait_ge(key_ready, 1)
                V.tensor_copy(key_i[0:EP, :], key[0:EP, 0:EC])
                V.tensor_copy(edge_i[0:EP, :], edge_f[0:EP, :])
                dve.wait_ge(key_mm, 1)
                link(V.tensor_tensor(dup[0:EP, :], key[0:EP, 0:EC], rank_ps[0:EP, 0:EC], ALU.is_equal))
                link(V.scalar_tensor_tensor(out=target[0:EP, :], in0=dup[0:EP, :], scalar=SKIP, in1=key[0:EP, 0:EC],
                                            op0=ALU.mult, op1=ALU.add))
                V.tensor_copy(target_i[0:EP, :], target[0:EP, :])
                dve.wait_ge(key_mm, 2)
                V.tensor_copy(keyT[0:EC, :], perm_ps[0:EC, 0:EP]).then_inc(keyT_ready, 1)
                dve.wait_ge(keyT_ready, 1)
                V.memset(zeros[:, 0:1], 0.0).then_inc(index_ready, 1)

            def sums_of(g, r, gp):
                ps = (rank_ps, perm_ps)[gp]
                for j in range(J):
                    at_least(dve, same_used, J * (g - 1) + j + 1, r if isinstance(r, int) else r * J)
                    ch = J * g + j if isinstance(r, int) else r * J + (J * g + j)
                    a = EP * (J * g + j) if isinstance(r, int) else r * (J * EP) + EP * (J * g + j)
                    V.tensor_scalar(same[0:EP, j, :], keyB[0:EP, bass.ds(a, EP)], key[0:EP, bass.ds(ch, 1)], None,
                                    ALU.is_equal).then_inc(same_ready, 1)

            def copy_sums(g, r, gp):
                ps = (rank_ps, perm_ps)[gp]
                at_least(dve, same_used, J * (g + 1), r if isinstance(r, int) else r * J)
                a = COLS * g if isinstance(r, int) else r * COLS + COLS * g
                V.tensor_copy(sumT[:, bass.ds(a, COLS)], ps[:, 0:COLS]).then_inc(sum_ready, 1)

            def prepass():
                dve.wait_ge(keyB_loaded, 16)
                for g in range(3):
                    sums_of(g, 0, g % 2)
                    copy_sums(g, 0, g % 2)
                with dve.Fori(0, (NE - 3) // 2) as h:
                    sums_of(3, h * 2, 1)
                    copy_sums(3, h * 2, 1)
                    sums_of(4, h * 2, 0)
                    copy_sums(4, h * 2, 0)
                dve.wait_ge(sum_ready, NE)
                last = sumT[:, :].rearrange("p (c e) -> p c e", e=EP)[:, :, EP - 1]
                V.tensor_copy(lastT[:], last).then_inc(last_ready, 1)
                dve.wait_ge(last_ready, 1)
                link(V.memset(last, 0.0))
                dve.wait_ge(last_mm, 1)
                V.tensor_copy(last_w[0:EC, :], perm_ps[0:EC, 0:P]).then_inc(last_w_ready, 1)

            def elu(c, m4, ps, neg_bias, exp_sb, h, min_ready, used, done):
                n = cols(c)
                at_least(dve, min_ready, c + 1, m4)
                at_least(dve, used, c - 1, m4)
                V.scalar_tensor_tensor(out=h[:, c % 2, 0:n], in0=ps[:, 0:n], scalar=neg_bias[:, 0:1],
                                       in1=exp_sb[:, c % 2, 0:n], op0=ALU.max, op1=ALU.add).then_inc(done, 1)

            def step(c, m4, m):
                if item_in(c) and is_edge(c):
                    at_least(dve, l1_ready, c - 1, m4)
                    if c == ND:
                        dve.wait_ge(last_w_ready, 1)
                    a = (c - ND) * COLS if isinstance(m, int) else m * (4 * COLS) + (c - ND) * COLS
                    V.tensor_scalar(carry[0:EC, c % 2, :], keyB[0:EC, bass.ds(a, COLS)], keyT[0:EC, EP - 1:EP], None,
                                    ALU.is_equal).then_inc(carry_ready, 1)
                if item_in(c - 1):
                    elu(c - 1, m4, l1_ps, neg_bias1, e1, h1, min1_ready, l2_ready, h1_ready)
                if item_in(c - 2):
                    elu(c - 2, m4, l2_ps, neg_bias2, e2, h2, min2_ready, z_ready, h2_ready)
                if item_in(c - 3):
                    i = c - 3
                    q = EP if is_edge(i) else P
                    at_least(dve, sq_ready, i + 1, m4)
                    at_least(dve, var_ready, i - 1, m4)
                    V.tensor_reduce(ssq[0:q, i % 2, :], sq[0:q, i % 2, :].rearrange("p (j f) -> p j f", j=J), AX_X,
                                    ALU.add).then_inc(ssq_ready, 1)
                if item_in(c - 4):
                    i = c - 4
                    k = i % SLOTS
                    q = EP if is_edge(i) else P
                    at_least(dve, rstd_ready, i + 1, m4)
                    if not is_edge(i):
                        at_least(dve, stored[k], 16 * (i // SLOTS), m * 16)
                    elif i - SLOTS < ND:
                        dve.wait_ge(stored[k], 16 * DENSE_ON[k])
                    else:
                        before_, r = slot_count(i, m)
                        at_least(dve, scattered[k], 64 * before_, r * 64)
                    V.tensor_tensor(o_sb[0:q, k, :].rearrange("p (j f) -> p j f", j=J),
                                    z_ps[0:q, i % 2, :].rearrange("p (j f) -> p j f", j=J),
                                    rstd[0:q, i % 2, :].rearrange("p (j a) -> p j a", a=1).to_broadcast([q, J, P]),
                                    ALU.mult).then_inc(o_ready, 1)

            constants()
            biases()
            digits()
            sort_pass(0)
            sort_pass(1)
            keys()
            walk(dve, step, at_mid=prepass)


_INS = ['x', 'src', 'edge_attr_128', 'L0_gnn_W0', 'L0_gnn_b0', 'L0_gnn_W2', 'L0_gnn_b2', 'L0_gnn_W3', 'L0_gnn_b3']


def kernel(**inputs):
    import numpy as _np
    import concourse.bacc as _bacc
    from concourse import mybir as _mybir
    from concourse.bass_utils import run_bass_kernel_spmd as _run

    nc = _bacc.Bacc("TRN2", target_bir_lowering=False, num_devices=1)
    arrays, args = {}, []
    for name in _INS:
        a = _np.ascontiguousarray(inputs[name])
        arrays[f"in_{name}_dram"] = a
        args.append(nc.dram_tensor(f"in_{name}_dram", a.shape, _mybir.dt.from_np(a.dtype), kind="ExternalInput").ap())
    key_rows = nc.dram_tensor("key_rows_dram", inputs['src'].shape, _mybir.dt.float32, kind="Internal").ap()
    out = nc.dram_tensor("out_0_dram", inputs['x'].shape, _mybir.dt.float32, kind="ExternalOutput").ap()
    gnn_resnorm(nc, *args, key_rows, out)
    r = _run(nc, [arrays], core_ids=[0])
    return r.results[0]["out_0_dram"]
```

```python
from contextlib import ExitStack

import concourse.bass as bass
from concourse import mybir

ALU = mybir.AluOpType
ACT = mybir.ActivationFunctionType
AX_X = mybir.AxisListType.X
F32 = mybir.dt.float32
BF16 = mybir.dt.bfloat16
I32 = mybir.dt.int32

P = 128
J = 4
EP = 125
DIG = 256
UNIT = 5
NPAY = 4
EPS = 1e-5
ROUND = 12582912.0
SKIP = 65536.0


def gnn_resnorm(nc, x, src, attr, W0, b0, W2, b2, W3, b3, key_rows, x_rows, out):
    N, F = x.shape
    E = src.shape[0]
    assert F == P and E % (EP * J) == 0 and N < DIG * DIG and N < SKIP
    EC = E // EP
    ROWS = J * P
    COLS = J * EP
    ND = -(-N // ROWS)
    NE = EC // J
    NI = ND + NE
    SLOTS = 4
    PASS = EC // UNIT
    LAG = 4
    STEPS = PASS + LAG
    FRONT = LAG * UNIT
    SC = FRONT + EC + FRONT

    HEAD = 4
    AT_PASS = (HEAD, HEAD + STEPS)
    AT_SUMS = HEAD + 2 * STEPS
    AT_GATHER = AT_SUMS + NE - 1
    AHEAD = 2
    LOOP_GATHER = (ND - 1 - AHEAD - AT_GATHER) // 4
    MID = AT_GATHER + 4 * LOOP_GATHER
    GATHER_END = AT_GATHER + NE - 1
    AT_EDGES = -(-(ND + 5) // 4) * 4
    LOOP_EDGES = (NI - AHEAD - AT_EDGES) // 4
    STEPS_END = NI + 5
    HIST_STEP = 2 * EC // HEAD
    assert STEPS % 4 == 0 and (NE - 1) % 4 == 0 and EC % UNIT == 0 and HIST_STEP % (2 * UNIT * UNIT) == 0
    assert MID <= GATHER_END <= AT_EDGES and GATHER_END - NE + 1 + AHEAD < ND

    with ExitStack() as ctx:
        def sb(name, shape, dt=F32):
            return ctx.enter_context(nc.sbuf_tensor(name, shape, dt))

        def psum(name):
            return ctx.enter_context(nc.psum_tensor(name, [P, J * P], F32))

        def sem(name):
            return ctx.enter_context(nc.semaphore(name))

        xT_ps = psum("xT_ps")
        l1_ps = psum("l1_ps")
        l2_ps = psum("l2_ps")
        z_ps = [psum(f"z_ps{k}") for k in range(2)]
        rank_ps = [psum(f"rank_ps{k}") for k in range(2)]
        perm_ps = psum("perm_ps")

        w0x = sb("w0x", [P, P])
        w0e = sb("w0e", [P, P])
        w2 = sb("w2", [P, P])
        w3 = sb("w3", [P, P])
        w3c = sb("w3c", [P, P])
        b_in = sb("b_in", [P, 3])
        w3_sum = sb("w3_sum", [P, 1])
        w3_mean = sb("w3_mean", [P, 1])
        minus_one = sb("minus_one", [P, 1])
        bias_x = sb("bias_x", [P, 1])
        bias1 = sb("bias1", [P, 1])
        neg_bias1 = sb("neg_bias1", [P, 1])
        bias2 = sb("bias2", [P, 1])
        neg_bias2 = sb("neg_bias2", [P, 1])
        neg_half = sb("neg_half", [P, J])
        diff_i = sb("diff_i", [P, P], I32)
        diff = sb("diff", [P, P])
        count_i = sb("count_i", [P, DIG], I32)
        count = sb("count", [P, DIG], BF16)
        prow_i = sb("prow_i", [P, 1], I32)
        ident = sb("ident", [P, P])
        center = sb("center", [P, P])
        before = sb("before", [P, P], BF16)
        not_before = sb("not_before", [P, P], BF16)
        ones = sb("ones", [P, P], BF16)
        next_row = sb("next_row", [P, P])
        next_col = sb("next_col", [P, P])
        zeros = sb("zeros", [P, DIG])
        zeros_b = sb("zeros_b", [P, J * P], BF16)

        src_i = sb("src_i", [P, EC], I32)
        digit_i = sb("digit_i", [P, 2, EC], I32)
        pay = sb("pay", [P, NPAY, SC])
        pay_last = sb("pay_last", [P, UNIT])
        onehot = sb("onehot", [P, 2 * UNIT, DIG], BF16)
        totals = sb("totals", [P, DIG])
        start = sb("start", [P, DIG])
        start_i = sb("start_i", [P, 3, DIG], I32)
        start_b = sb("start_b", [P, 2, 2, DIG], BF16)
        picked = sb("picked", [P, 2, DIG])
        pos = sb("pos", [P, SC])
        quot = sb("quot", [P, SC])
        pos_col = sb("pos_col", [P, SC])
        pos_row = sb("pos_row", [P, SC])
        row_hot = sb("row_hot", [P, 4 * UNIT, EP], BF16)
        col_hot = sb("col_hot", [P, 4 * UNIT, EC], BF16)
        col_pay = sb("col_pay", [P, 2 * UNIT, NPAY, EC], BF16)

        key = sb("key", [P, EC + 1])
        key_i = sb("key_i", [P, EC], I32)
        edge_f = sb("edge_f", [P, EC])
        edge_i = sb("edge_i", [P, EC], I32)
        dup = sb("dup", [P, EC])
        target = sb("target", [P, EC])
        target_i = sb("target_i", [P, EC], I32)
        keyT = sb("keyT", [P, EP])
        keyB = sb("keyB", [P, E])
        attr_sb = sb("attr_sb", [P, 2, J, P])
        same = sb("same", [P, 2 * J, EP])
        sumT = sb("sumT", [P, E])
        lastT = sb("lastT", [P, EC])
        last_w = sb("last_w", [P, P])
        carry = sb("carry", [P, 2, COLS])
        attr_idx = sb("attr_idx", [P, 2, J], I32)
        x_idx = sb("x_idx", [P, 2, J], I32)
        out_idx = sb("out_idx", [P, SLOTS, J], I32)
        xg_sb = sb("xg_sb", [P, 2, J * P])

        x_sb = sb("x_sb", [P, SLOTS, J * P])
        xT = sb("xT", [P, SLOTS, J * P])
        e1 = sb("e1", [P, J * P])
        e2 = sb("e2", [P, J * P])
        m1 = sb("m1", [P, J * P])
        m2 = sb("m2", [P, J * P])
        h1 = sb("h1", [P, 2, J * P])
        h2 = sb("h2", [P, 2, J * P])
        sq = sb("sq", [P, J, P])
        ssq = sb("ssq", [P, 2, J])
        var_eps = sb("var_eps", [P, 2, J])
        rstd = sb("rstd", [P, 2, J])
        o_sb = sb("o_sb", [P, SLOTS, J * P])

        weights_loaded = sem("weights_loaded")
        src_loaded = sem("src_loaded")
        consts_made = sem("consts_made")
        dve_chain = sem("dve_chain")
        pool_waits = sem("pool_waits")
        sp_waits = sem("sp_waits")
        setup_mm = sem("setup_mm")
        b3_ready = sem("b3_ready")
        biases_ready = sem("biases_ready")
        onehot_ready = sem("onehot_ready")
        onehot_free = sem("onehot_free")
        hist_done = sem("hist_done")
        start_ready = sem("start_ready")
        rank_ready = sem("rank_ready")
        rank_free = sem("rank_free")
        place_known = sem("place_known")
        col_ready = sem("col_ready")
        pay_act = sem("pay_act")
        pay_pool = sem("pay_pool")
        pay_last_ready = sem("pay_last_ready")
        place_free = sem("place_free")
        permuted = sem("permuted")
        pay_ready = sem("pay_ready")
        key_ready = sem("key_ready")
        key_mm = sem("key_mm")
        keyT_ready = sem("keyT_ready")
        keys_stored = sem("keys_stored")
        keyB_loaded = sem("keyB_loaded")
        index_ready = sem("index_ready")
        attr_idx_ready = sem("attr_idx_ready")
        attr_loaded = [sem(f"attr_loaded{k}") for k in range(2)]
        same_ready = sem("same_ready")
        same_free = sem("same_free")
        sum_ready = sem("sum_ready")
        last_ready = sem("last_ready")
        last_mm = sem("last_mm")
        last_w_ready = sem("last_w_ready")
        carry_ready = sem("carry_ready")

        x_loaded = [sem(f"x_loaded{k}") for k in range(SLOTS)]
        x_gathered = [sem(f"x_gathered{k}") for k in range(2)]
        x_stashed = [sem(f"x_stashed{k}") for k in range(2)]
        x_idx_ready = sem("x_idx_ready")
        out_idx_ready = sem("out_idx_ready")
        xT_ps_ready = sem("xT_ps_ready")
        xT_ready = sem("xT_ready")
        l1_ready = sem("l1_ready")
        exp1_ready = sem("exp1_ready")
        min1_ready = sem("min1_ready")
        h1_ready = sem("h1_ready")
        l2_ready = sem("l2_ready")
        exp2_ready = sem("exp2_ready")
        min2_ready = sem("min2_ready")
        h2_ready = sem("h2_ready")
        z_ready = sem("z_ready")
        ssq_ready = sem("ssq_ready")
        var_ready = sem("var_ready")
        rstd_ready = sem("rstd_ready")
        o_ready = sem("o_ready")
        stored = [sem(f"stored{k}") for k in range(SLOTS)]
        scattered = [sem(f"scattered{k}") for k in range(SLOTS)]

        DENSE_ON = [len(range(k, ND, SLOTS)) for k in range(SLOTS)]

        def at_least(eng, semaphore, const, reg=0):
            if isinstance(reg, int):
                if const + reg > 0:
                    eng.wait_ge(semaphore, const + reg)
            else:
                assert const >= 0, const
                eng.wait_ge(semaphore, reg + const)

        def carried_at_least(eng, carrier, semaphore, const, reg=0):
            at_least(eng, semaphore, const, reg)
            if not isinstance(reg, int):
                eng.sem_inc(carrier, 1)

        def cut(ap, const, reg, size):
            if isinstance(reg, int):
                return ap[:, const + reg:const + reg + size]
            return ap[:, bass.ds(reg + const, size)]

        def times(reg, k):
            return reg * k

        def is_edge(c):
            return c >= ND

        def item_in(c):
            return 0 <= c < NI

        def cols(c):
            return COLS if is_edge(c) else ROWS

        def rows(c):
            return slice(0, EP if is_edge(c) else P)

        def none(*_):
            return []

        def walk(eng, step, hist=none, sort_batch=none, finish=none, first=none, sums=none, middle=none,
                 gather=none, after_gather=none, last=none):
            for c in range(HEAD):
                step(c, 0, 0, hist(c))
            for n in range(2):
                finish(n)
                with eng.Fori(0, STEPS // 4) as m:
                    for u in range(4):
                        step(AT_PASS[n] + u, m * 4, m, sort_batch(n, u, m * 4))
            finish(2)
            first()
            with eng.Fori(0, (NE - 1) // 4) as m:
                for u in range(4):
                    step(AT_SUMS + u, m * 4, m, sums(u, m * 4))
            middle()
            with eng.Fori(0, LOOP_GATHER) as m:
                for u in range(4):
                    step(AT_GATHER + u, m * 4, m, gather(u, m * 4))
            for c in range(MID, AT_EDGES):
                if c == GATHER_END:
                    after_gather()
                if c == ND + 5:
                    last()
                step(c, 0, 0, gather(c - AT_GATHER, 0) if c < GATHER_END else [])
            if GATHER_END == AT_EDGES:
                after_gather()
            if AT_EDGES == ND + 5:
                last()
            with eng.Fori(0, LOOP_EDGES) as m:
                for u in range(4):
                    step(AT_EDGES + u, m * 4, m, [])
            for c in range(AT_EDGES + 4 * LOOP_EDGES, STEPS_END):
                step(c, 0, 0, [])

        def run(parts, beside):
            beside = list(beside)
            for part in parts:
                part()
                if beside:
                    beside.pop(0)()
            for part in beside:
                part()

        block = ctx.enter_context(nc.Block())

        @block.sync
        def _(sp):
            sp.dma_start(src_i[0:EP, :], src.rearrange("(p c) -> p c", p=EP)).then_inc(src_loaded, 16)
            sp.dma_start(w0x[:], W0[0:P, :]).then_inc(weights_loaded, 16)
            sp.dma_start(w0e[:], W0[P:2 * P, :]).then_inc(weights_loaded, 16)
            sp.dma_start(w2[:], W2[:, :]).then_inc(weights_loaded, 16)
            sp.dma_start(w3[:], W3[:, :]).then_inc(weights_loaded, 16)
            for k, b in enumerate((b0, b2, b3)):
                sp.dma_start(b_in[:, k:k + 1], b.rearrange("(p a) -> p a", a=1)).then_inc(weights_loaded, 16)

            def rows_of(ap, c, m):
                if c == ND - 1:
                    part = ap[N - ROWS:N, :]
                elif isinstance(m, int):
                    part = ap[c * ROWS:(c + 1) * ROWS, :]
                else:
                    part = ap[bass.ds(m * (4 * ROWS) + c * ROWS, ROWS), :]
                return part.rearrange("(p j) f -> p (j f)", p=P)

            def x_rows_of(e, r):
                part = x_rows[bass.ds(r * EP + e * EP, EP), :] if not isinstance(r, int) else x_rows[e * EP:(e + 1) * EP, :]
                return part

            def stash(e, r):
                carried_at_least(sp, sp_waits, x_gathered[e % 2], 64 * (e // 2 + 1), times(r, 32))
                sp.dma_start(x_rows_of(e, r), xg_sb[0:EP, e % 2, :]).then_inc(x_stashed[e % 2], 16)

            def load(c, m4, m):
                k = c % SLOTS
                if not item_in(c):
                    return
                carried_at_least(sp, sp_waits, xT_ps_ready, c - SLOTS + 1, m4)
                if not is_edge(c):
                    sp.dma_start(x_sb[:, k, :], rows_of(x, c, m)).then_inc(x_loaded[k], 16)
                else:
                    e = c - ND
                    carried_at_least(sp, sp_waits, x_stashed[e % 2], 16 * (e // 2 + 1), times(m, 32))
                    sp.dma_start(x_sb[0:EP, k, :], x_rows_of(e, m4)).then_inc(x_loaded[k], 16)

            def step(c, m4, m, beside):
                load(c + AHEAD, m4, m)
                i = c - 4
                if 0 <= i < ND:
                    carried_at_least(sp, sp_waits, o_ready, i + 1, m4)
                    if i == ND - 1:
                        sp.wait_ge(stored[(i - 1) % SLOTS], 16 * DENSE_ON[(i - 1) % SLOTS])
                    sp.dma_start(rows_of(out, i, m), o_sb[:, i % SLOTS, :]).then_inc(stored[i % SLOTS], 16)
                for part in beside:
                    part()

            for c in range(AHEAD):
                load(c, 0, 0)
            walk(sp, step, gather=lambda e, r: [lambda: stash(e, r)], after_gather=lambda: stash(NE - 1, 0))
            for k in range(SLOTS):
                sp.wait_ge(stored[k], 16 * DENSE_ON[k])

        @block.gpsimd
        def _(pool):
            nc.gpsimd.iota(diff_i[:], pattern=[[1, P]], base=0, channel_multiplier=-1).then_inc(consts_made, 1)
            nc.gpsimd.iota(count_i[:], pattern=[[1, DIG]], base=0, channel_multiplier=0).then_inc(consts_made, 1)
            nc.gpsimd.iota(prow_i[:], pattern=[[0, 1]], base=0, channel_multiplier=1).then_inc(consts_made, 1)
            pool.wait_ge(biases_ready, 1)

            def sort_batch(n, t, r):
                def one(u):
                    def do():
                        d = n * STEPS * UNIT + UNIT * t + u
                        if u == 0:
                            carried_at_least(pool, pool_waits, pay_pool, d + UNIT, times(r, UNIT))
                            nc.gpsimd.tensor_copy(pay_last[0:EP, :], cut(pay[0:EP, NPAY - 1, :], FRONT + UNIT * (t - 3),
                                                                         times(r, UNIT), UNIT)).then_inc(pay_last_ready, 1)
                            carried_at_least(pool, pool_waits, pay_last_ready, n * STEPS + t + 1, r)
                        carried_at_least(pool, pool_waits, col_ready, d + 1, times(r, UNIT))
                        carried_at_least(pool, pool_waits, place_free, d + UNIT + 1, times(r, UNIT))
                        nc.gpsimd.tensor_scalar(col_pay[0:EP, UNIT * ((t - 3) % 2) + u, NPAY - 1, :],
                                                col_hot[0:EP, UNIT * ((t - 3) % 4) + u, :],
                                                pay_last[0:EP, u:u + 1], None, ALU.mult).then_inc(pay_pool, 1)
                    return do
                return [one(u) for u in range(UNIT)]

            def gather_attr(g, r):
                gp = g % 2
                at_least(pool, attr_loaded[gp], 64 * (g // 2), times(r, 32))
                carried_at_least(pool, pool_waits, same_free, 2 * J + J * (g - 1), times(r, J))
                nc.gpsimd.tensor_copy(attr_idx[0:EP, gp, :], cut(edge_i[0:EP, :], J * g, times(r, J), J))\
                    .then_inc(attr_idx_ready, 1)
                carried_at_least(pool, pool_waits, attr_idx_ready, g + 1, r)
                for j in range(J):
                    nc.gpsimd.indirect_dma_start(
                        out=attr_sb[0:EP, gp, j, :], out_offset=None, in_=attr[:, :],
                        in_offset=bass.IndirectOffsetOnAxis(ap=attr_idx[0:EP, gp, j:j + 1], axis=0),
                    ).then_inc(attr_loaded[gp], 16)

            def gather_x(e, r):
                gp = e % 2
                at_least(pool, x_stashed[gp], 16 * (e // 2), times(r, 8))
                nc.gpsimd.tensor_copy(x_idx[0:EP, gp, :], cut(key_i[0:EP, :], J * e, times(r, J), J))\
                    .then_inc(x_idx_ready, 1)
                carried_at_least(pool, pool_waits, x_idx_ready, e + 1, r)
                for j in range(J):
                    nc.gpsimd.indirect_dma_start(
                        out=xg_sb[0:EP, gp, j * P:(j + 1) * P], out_offset=None, in_=x[:, :],
                        in_offset=bass.IndirectOffsetOnAxis(ap=x_idx[0:EP, gp, j:j + 1], axis=0),
                    ).then_inc(x_gathered[gp], 16)

            def scatter_out(c, m4, m):
                k = c % SLOTS
                e = c - ND
                at_least(pool, scattered[k], 64 * (e // SLOTS), times(m, 64))
                carried_at_least(pool, pool_waits, o_ready, c + 1, m4)
                nc.gpsimd.tensor_copy(out_idx[0:EP, k, :], cut(target_i[0:EP, :], e * J, times(m4, J), J))\
                    .then_inc(out_idx_ready, 1)
                carried_at_least(pool, pool_waits, out_idx_ready, e + 1, m4)
                for j in range(J):
                    nc.gpsimd.indirect_dma_start(
                        out=out[:, :], out_offset=bass.IndirectOffsetOnAxis(ap=out_idx[0:EP, k, j:j + 1], axis=0),
                        in_=o_sb[0:EP, k, j * P:(j + 1) * P], in_offset=None,
                        bounds_check=N - 1, oob_is_err=False,
                    ).then_inc(scattered[k], 16)

            def step(c, m4, m, beside):
                for part in beside:
                    part()
                if item_in(c - 5) and is_edge(c - 5):
                    scatter_out(c - 5, m4, m)
                if item_in(c - 3):
                    i = c - 3
                    q = rows(i)
                    carried_at_least(pool, pool_waits, ssq_ready, i + 1, m4)
                    nc.gpsimd.tensor_scalar(var_eps[q, i % 2, :], ssq[q, i % 2, :], EPS, None, ALU.add).then_inc(var_ready, 1)
                    at_least(pool, var_ready, i + 1, m4)
                    carried_at_least(pool, pool_waits, o_ready, i - 1, m4)
                    nc.gpsimd.tensor_tensor(rstd[q, i % 2, :], var_eps[q, i % 2, :], neg_half[q, :], ALU.pow)\
                        .then_inc(rstd_ready, 1)

            def finish(n):
                if n < 2:
                    pool.wait_ge(pay_ready, 2 * n + 1)

            def first():
                pool.wait_ge(keyT_ready, 1)
                pool.dma_start(key_rows.rearrange("(c e) -> c e", e=EP), keyT[0:EC, :]).then_inc(keys_stored, 16)
                pool.wait_ge(index_ready, 1)
                gather_attr(0, 0)
                pool.wait_ge(keys_stored, 16)
                pool.dma_start(keyB[:], key_rows.rearrange("(a e) -> a e", a=1).to_broadcast([P, E])).then_inc(keyB_loaded, 16)

            def last():
                for k in range(SLOTS):
                    pool.wait_ge(stored[k], 16 * DENSE_ON[k])

            walk(pool, step, finish=finish, first=first, last=last,
                 sort_batch=sort_batch,
                 sums=lambda g, r: [lambda: gather_attr(g + 1, r)],
                 middle=lambda: gather_x(0, 0),
                 gather=lambda e, r: [lambda: gather_x(e + 1, r)])
            for k in range(SLOTS):
                pool.wait_ge(scattered[k], 64 * len([i for i in range(ND, NI) if i % SLOTS == k]))

        @block.tensor
        def _(pe):
            T = nc.tensor

            def small_products():
                pe.sem_inc(onehot_free, UNIT)
                pe.sem_inc(place_free, 2 * UNIT)
                pe.sem_inc(same_free, 2 * J)
                pe.sem_inc(rank_ready, 2)
                pe.sem_inc(col_ready, UNIT)
                pe.sem_inc(pay_act, UNIT)
                pe.sem_inc(pay_pool, UNIT)
                pe.wait_ge(weights_loaded, 16 * 7)
                pe.wait_ge(b3_ready, 1)
                T.matmul(l1_ps[:, 0:1], w2[:], minus_one[:], start=True, stop=True)
                T.matmul(l2_ps[:, 0:1], center[:], b_in[:, 2:3], start=True, stop=False)
                T.matmul(l2_ps[:, 0:1], w3c[:], minus_one[:], start=False, stop=True).then_inc(setup_mm, 1)
                pe.wait_ge(b3_ready, 2)
                T.matmul(z_ps[0][:, 0:1], w0x[:], bias_x[:], start=True, stop=True).then_inc(setup_mm, 1)
                pe.wait_ge(biases_ready, 1)

            def clear(bank, first):
                return T.matmul(bank[0:EP, :], ones[0:EP, 0:EP], zeros_b[0:EP, :], start=first, stop=not first,
                                skip_group_check=True)

            def hist(c):
                per, half = HIST_STEP, HEAD // 2
                bank = rank_ps[c // half]

                def piece(p):
                    def do():
                        if c % half == 0 and p == 0:
                            clear(bank, True)
                        with pe.Fori(0, per // UNIT // UNIT) as m:
                            for u in range(UNIT):
                                at_least(pe, onehot_ready, c * per + p * (per // UNIT) + u + 1, m * UNIT)
                                T.matmul(bank[0:EP, 0:DIG], ones[0:EP, 0:EP], onehot[0:EP, u, :], start=False, stop=False,
                                         skip_group_check=True).then_inc(onehot_free, 1)
                        if c % half == half - 1 and p == UNIT - 1:
                            clear(bank, False).then_inc(hist_done, 1)
                    return do
                return [piece(p) for p in range(UNIT)]

            def sort_batch(n, t, r):
                reg = times(r, UNIT)

                def rank(u):
                    d = UNIT * t + u
                    bank = rank_ps[d % 2][0:EP, 0:DIG]
                    slot = d + UNIT
                    at_least(pe, onehot_ready, 2 * EC + (n * STEPS - 1) * UNIT + d + 1, reg)
                    at_least(pe, rank_free, n * STEPS * UNIT + d + 1, reg)
                    for weights, back in ((not_before, 2), (ones, 1), (before, 0)):
                        mm = T.matmul(bank, weights[0:EP, 0:EP], onehot[0:EP, (slot - back) % (2 * UNIT), :],
                                      start=False, stop=False, skip_group_check=True)
                    mm.then_inc(rank_ready, 1)

                def place(u):
                    d = n * STEPS * UNIT + UNIT * t + u
                    at_least(pe, pay_act, d + 1, reg)
                    at_least(pe, pay_pool, d + 1, reg)
                    T.matmul(perm_ps[0:EP, 0:NPAY * EC], row_hot[0:EP, UNIT * (t % 4) + u, :],
                             col_pay[0:EP, UNIT * (t % 2) + u, :, :].rearrange("p k c -> p (k c)"),
                             start=False, stop=False, skip_group_check=True).then_inc(place_free, 1)

                return [lambda u=u: (rank(u), place(u)) for u in range(UNIT)]

            def finish(n):
                if n > 0:
                    clear(perm_ps, False).then_inc(permuted, 1)
                if n < 2:
                    pe.wait_ge(start_ready, 1)
                    pe.wait_ge(rank_free, n * STEPS * UNIT + 1)
                    for bank in rank_ps:
                        for part in range(2):
                            mm = T.matmul(bank[0:EP, 0:DIG], ones[0:1, 0:EP], start_b[0:1, n, part, :],
                                          start=(part == 0), stop=False, skip_group_check=True)
                    mm.then_inc(rank_ready, 1)
                    pe.wait_ge(pay_ready, 2 * n + 2)
                    clear(perm_ps, True)

            def first():
                pe.wait_ge(key_ready, 1)
                T.matmul(rank_ps[0][0:EP, 0:EC], next_row[0:EP, 0:EP], key[0:EP, 0:EC], start=True, stop=False)
                T.matmul(rank_ps[0][0:EP, 0:EC], next_col[0:EP, 0:EP], key[0:EP, 1:EC + 1],
                         start=False, stop=True).then_inc(key_mm, 1)
                T.transpose(perm_ps[0:EC, 0:EP], key[0:EP, 0:EC], ident[0:EP, 0:EP]).then_inc(key_mm, 1)
                pe.wait_ge(index_ready, 1)

            def sums(g, r):
                def one(j):
                    def do():
                        if j == 0:
                            at_least(pe, attr_loaded[g % 2], 64 * (g // 2 + 1), times(r, 32))
                            at_least(pe, sum_ready, g, r)
                        at_least(pe, same_ready, J * g + j + 1, times(r, J))
                        T.matmul(rank_ps[g % 2][:, j * EP:(j + 1) * EP], attr_sb[0:EP, g % 2, j, :],
                                 same[0:EP, J * (g % 2) + j, :],
                                 start=(j == 0), stop=(j == J - 1), skip_group_check=True).then_inc(same_free, 1)
                    return do
                return [one(j) for j in range(J)]

            def middle():
                for part in sums(NE - 1, 0):
                    part()
                pe.wait_ge(last_ready, 1)
                T.matmul(perm_ps[0:EC, 0:P], lastT[:], w0e[:], start=True, stop=True).then_inc(last_mm, 1)

            def layer1(c, m4, m):
                n = cols(c)
                at_least(pe, xT_ready, c + 1, m4)
                at_least(pe, h1_ready, c, m4)
                ps = l1_ps[:, 0:n]
                if not is_edge(c):
                    T.matmul(ps, w0x[:], xT[:, c % SLOTS, 0:n], start=True, stop=True).then_inc(l1_ready, 1)
                    return
                e = c - ND
                T.matmul(ps, w0x[:], xT[:, c % SLOTS, 0:n], start=True, stop=False)
                T.matmul(ps, w0e[:], cut(sumT[:, :], e * COLS, times(m, 4 * COLS), COLS), start=False, stop=False)
                at_least(pe, carry_ready, e + 1, m4)
                T.matmul(ps, last_w[0:EC, :], carry[0:EC, c % 2, :], start=False, stop=True).then_inc(l1_ready, 1)

            def turn(c, m4, m):
                q = EP if is_edge(c) else P
                at_least(pe, x_loaded[c % SLOTS], 16 * (c // SLOTS + 1), times(m, 16))
                at_least(pe, xT_ready, c, m4)
                for j in range(J):
                    mm = T.transpose(xT_ps[:, j * q:(j + 1) * q], x_sb[0:q, c % SLOTS, j * P:(j + 1) * P],
                                     ident[0:q, 0:q])
                mm.then_inc(xT_ps_ready, 1)

            def layer2(c, m4):
                n = cols(c)
                at_least(pe, h1_ready, c + 1, m4)
                at_least(pe, h2_ready, c, m4)
                T.matmul(l2_ps[:, 0:n], w2[:], h1[:, c % 2, 0:n], start=True, stop=True).then_inc(l2_ready, 1)

            def layer3(c, m4):
                q = EP if is_edge(c) else P
                at_least(pe, h2_ready, c + 1, m4)
                at_least(pe, o_ready, c - 1, m4)
                for j in range(J):
                    z = z_ps[c % 2][0:q, j * P:(j + 1) * P]
                    T.matmul(z, xT[:, c % SLOTS, j * q:(j + 1) * q], center[:], start=True, stop=False)
                    mm = T.matmul(z, h2[:, c % 2, j * q:(j + 1) * q], w3c[:], start=False, stop=True)
                mm.then_inc(z_ready, 1)

            def step(c, m4, m, beside):
                parts = []
                if item_in(c - 1):
                    parts.append(lambda: layer1(c - 1, m4, m))
                if item_in(c):
                    parts.append(lambda: turn(c, m4, m))
                if item_in(c - 2):
                    parts.append(lambda: layer2(c - 2, m4))
                if item_in(c - 3):
                    parts.append(lambda: layer3(c - 3, m4))
                run(parts, beside)

            small_products()
            walk(pe, step, hist=hist, sort_batch=sort_batch, finish=finish, first=first, sums=sums, middle=middle)

        @block.scalar
        def _(act):
            A = nc.scalar

            def sort_batch(n, t, r):
                def one(u):
                    def do():
                        d = n * STEPS * UNIT + UNIT * t + u
                        at_least(act, col_ready, d + 1, times(r, UNIT))
                        at_least(act, place_free, d + UNIT + 1, times(r, UNIT))
                        for k in range(NPAY - 1):
                            t_ = A.activation(col_pay[0:EP, UNIT * ((t - 3) % 2) + u, k, :],
                                              col_hot[0:EP, UNIT * ((t - 3) % 4) + u, :], ACT.Copy,
                                              scale=cut(pay[0:EP, k, :], FRONT + UNIT * (t - 3) + u, times(r, UNIT), 1))
                        t_.then_inc(pay_act, 1)
                    return do
                return [one(u) for u in range(UNIT)]

            def finish(n):
                if n < 2:
                    act.wait_ge(pay_ready, 2 * n + 1)

            def copy_sums(g, r):
                def do():
                    at_least(act, same_free, 2 * J + J * (g + 1), times(r, J))
                    A.copy(cut(sumT[:, :], COLS * g, times(r, COLS), COLS), rank_ps[g % 2][:, 0:COLS]).then_inc(sum_ready, 1)
                return [list] * J + [do]

            def turned(c, m4):
                n = cols(c)
                at_least(act, xT_ps_ready, c + 1, m4)
                at_least(act, z_ready, c - SLOTS + 1, m4)
                A.activation(xT[:, c % SLOTS, 0:n], xT_ps[:, 0:n], ACT.Identity, bias=bias_x[:, 0:1]).then_inc(xT_ready, 1)

            def exp(c, m4, ps, ready, bias, e, free, done):
                n = cols(c)
                at_least(act, ready, c + 1, m4)
                at_least(act, free, c, m4)
                A.activation(e[:, 0:n], ps[:, 0:n], ACT.Exp, bias=bias[:, 0:1]).then_inc(done, 1)

            def squares(c, m4):
                q = rows(c)
                at_least(act, z_ready, c + 1, m4)
                at_least(act, rstd_ready, c - 1, m4)
                at_least(act, ssq_ready, c, m4)
                for j in range(J):
                    t = A.activation(sq[q, j, :], z_ps[c % 2][q, j * P:(j + 1) * P], ACT.Square,
                                     scale=float(P) ** -0.5, accum_out=ssq[q, c % 2, j:j + 1])
                t.then_inc(ssq_ready, 1)

            def step(c, m4, m, beside):
                parts = []
                if item_in(c - 1):
                    parts.append(lambda: exp(c - 1, m4, l1_ps, l1_ready, bias1, e1, min1_ready, exp1_ready))
                if item_in(c):
                    parts.append(lambda: turned(c, m4))
                if item_in(c - 2):
                    parts.append(lambda: exp(c - 2, m4, l2_ps, l2_ready, bias2, e2, min2_ready, exp2_ready))
                if item_in(c - 3):
                    parts.append(lambda: squares(c - 3, m4))
                run(parts, beside)

            act.wait_ge(biases_ready, 1)
            walk(act, step, finish=finish, sort_batch=sort_batch, sums=copy_sums,
                 middle=lambda: copy_sums(NE - 1, 0)[-1]())

        @block.vector
        def _(dve):
            chain = [0]

            def link(ins):
                chain[0] += 1
                ins.then_inc(dve_chain, 1)
                dve.wait_ge(dve_chain, chain[0])

            V = nc.vector

            def constants():
                dve.wait_ge(consts_made, 3)
                V.memset(zeros[:], 0.0)
                V.memset(minus_one[:], -1.0)
                V.memset(neg_half[:], -0.5)
                V.memset(ones[:], 1.0)
                V.memset(pay[:], 0.0)
                V.memset(pos[:], 0.0)
                V.memset(onehot[:], 0.0)
                V.memset(row_hot[:], 0.0)
                V.memset(col_hot[:], 0.0)
                V.memset(col_pay[:], 0.0)
                V.memset(zeros_b[:], 0.0)
                V.memset(key[:], -1.0)
                V.tensor_copy(diff[:], diff_i[:])
                link(V.tensor_copy(count[:], count_i[:]))
                V.tensor_scalar(before[:], diff[:], 0.0, None, ALU.is_gt)
                V.tensor_scalar(not_before[:], diff[:], 0.0, None, ALU.is_le)
                V.tensor_scalar(next_row[:], diff[:], -1.0, None, ALU.is_equal)
                V.tensor_scalar(next_col[:], diff[:], float(EP - 1), None, ALU.is_equal)
                V.tensor_scalar(ident[:], diff[:], 0.0, None, ALU.is_equal)
                V.tensor_scalar(center[:], diff[:], 0.0, -1.0 / P, ALU.is_equal, ALU.add)
                V.tensor_copy(pay[0:EP, 2, FRONT:FRONT + EC], prow_i[0:EP, 0:1].to_broadcast([EP, EC]))
                link(V.tensor_copy(pay[0:EP, 3, FRONT:FRONT + EC], count_i[0:EP, 0:EC]))

            def biases():
                dve.wait_ge(weights_loaded, 16 * 7)
                link(V.reduce_sum(w3_sum[:], w3[:], AX_X))
                link(V.tensor_scalar(w3_mean[:], w3_sum[:], 1.0 / P, None, ALU.mult))
                V.tensor_scalar(w3c[:], w3[:], w3_mean[:, 0:1], None, ALU.subtract).then_inc(b3_ready, 1)
                dve.wait_ge(setup_mm, 1)
                V.tensor_copy(bias_x[:], l2_ps[:, 0:1]).then_inc(b3_ready, 1)
                link(V.tensor_scalar(bias2[:], l1_ps[:, 0:1], b_in[:, 1:2], None, ALU.add))
                V.tensor_scalar(neg_bias2[:], bias2[:], -1.0, None, ALU.mult)
                dve.wait_ge(setup_mm, 2)
                link(V.tensor_tensor(bias1[:], b_in[:, 0:1], z_ps[0][:, 0:1], ALU.subtract))
                link(V.tensor_scalar(neg_bias1[:], bias1[:], -1.0, None, ALU.mult))
                V.memset(picked[:], 0.0).then_inc(biases_ready, 1)

            def digits():
                dve.wait_ge(src_loaded, 16)
                V.tensor_scalar(digit_i[0:EP, 0, :], src_i[0:EP, :], 8, None, ALU.logical_shift_right)
                link(V.tensor_scalar(digit_i[0:EP, 1, :], src_i[0:EP, :], DIG - 1, None, ALU.bitwise_and))
                link(V.tensor_copy(pay[0:EP, 0:2, FRONT:FRONT + EC], digit_i[0:EP, :, :]))

            def make_onehot(d, const, reg, slot):
                V.tensor_scalar(onehot[0:EP, slot, :], count[0:EP, :], cut(pay[0:EP, d, :], const, reg, 1), None,
                                ALU.is_equal).then_inc(onehot_ready, 1)

            def hist(c):
                per, half = HIST_STEP, HEAD // 2

                def piece(p):
                    def do():
                        with dve.Fori(0, per // UNIT // UNIT) as m:
                            for u in range(UNIT):
                                d = p * (per // UNIT) + u
                                at_least(dve, onehot_free, c * per + d + 1, m * UNIT)
                                make_onehot(1 - c // half, FRONT + (c % half) * per + d, m * UNIT, u)
                    return do
                return [piece(p) for p in range(UNIT)]

            def starts():
                for n in range(2):
                    dve.wait_ge(hist_done, n + 1)
                    tot = rank_ps[n][0:EP, 0:DIG]
                    link(V.tensor_tensor_scan(totals[0:EP, :], tot, zeros[0:EP, :], 0.0, ALU.add, ALU.add))
                    link(V.tensor_tensor(start[0:EP, :], totals[0:EP, :], tot, ALU.subtract))
                    link(V.tensor_copy(start_i[0:EP, 0, :], start[0:EP, :]))
                    V.tensor_scalar(start_i[0:EP, 1, :], start_i[0:EP, 0, :], 127, None, ALU.bitwise_and)
                    link(V.tensor_scalar(start_i[0:EP, 2, :], start_i[0:EP, 0, :], 65536 - 128, None, ALU.bitwise_and))
                    link(V.tensor_copy(start_b[0:EP, n, :, :], start_i[0:EP, 1:3, :]))
                dve.sem_inc(rank_free, 1)
                dve.sem_inc(start_ready, 1)

            def sort_batch(n, t, r):
                reg, r3 = times(r, UNIT), times(r, 3)
                d0 = n * STEPS * UNIT + UNIT * t
                k = 3 * (n * STEPS + t)
                old = FRONT + UNIT * (t - 2)

                def digit(u):
                    at_least(dve, rank_ready, n + d0 + u + 1, reg)
                    make_onehot(1 - n, FRONT + UNIT * t + u, reg, UNIT * (t % 2) + u)

                def extract(u):
                    x = UNIT * t + u + 1
                    at_least(dve, rank_ready, n * (STEPS * UNIT + 1) + x + 3, reg)
                    V.scalar_tensor_tensor(out=picked[0:EP, x % 2, :], in0=rank_ps[(x - 1) % 2][0:EP, 0:DIG], scalar=0.0,
                                           in1=onehot[0:EP, (x - 1 + UNIT) % (2 * UNIT), :], op0=ALU.add, op1=ALU.mult,
                                           accum_out=cut(pos[0:EP, :], FRONT + UNIT * (t - 1) + u, reg, 1))\
                        .then_inc(rank_free, 1)

                def quotient():
                    at_least(dve, rank_free, d0 + 2, reg)
                    V.tensor_scalar(cut(quot[0:EP, :], old, reg, UNIT), cut(pos[0:EP, :], old, reg, UNIT),
                                    1.0 / EP, -(EP // 2) / EP, ALU.mult, ALU.add).then_inc(place_known, 1)

                def column():
                    at_least(dve, place_known, k + 1, r3)
                    V.tensor_scalar(cut(pos_col[0:EP, :], old, reg, UNIT), cut(quot[0:EP, :], old, reg, UNIT),
                                    ROUND, ROUND, ALU.add, ALU.subtract).then_inc(place_known, 1)

                def row():
                    at_least(dve, place_known, k + 2, r3)
                    V.scalar_tensor_tensor(out=cut(pos_row[0:EP, :], old, reg, UNIT), in0=cut(pos_col[0:EP, :], old, reg, UNIT),
                                           scalar=-float(EP), in1=cut(pos[0:EP, :], old, reg, UNIT),
                                           op0=ALU.mult, op1=ALU.add).then_inc(place_known, 1)

                def hots(u):
                    if u == 0:
                        at_least(dve, place_known, k + 3, r3)
                    at_least(dve, place_free, d0 + u + 1, reg)
                    slot = UNIT * ((t - 2) % 4) + u
                    V.tensor_scalar(row_hot[0:EP, slot, :], count[0:EP, 0:EP], cut(pos_row[0:EP, :], old + u, reg, 1), None,
                                    ALU.is_equal)
                    V.tensor_scalar(col_hot[0:EP, slot, :], count[0:EP, 0:EC], cut(pos_col[0:EP, :], old + u, reg, 1), None,
                                    ALU.is_equal).then_inc(col_ready, 1)

                return [lambda: (extract(-1), digit(0), quotient(), digit(1), column()),
                        lambda: (extract(0), row(), digit(2), hots(0)),
                        lambda: (extract(1), hots(1)),
                        lambda: (extract(2), digit(3), hots(2)),
                        lambda: (extract(3), digit(4), hots(3), hots(4))]

            def finish(n):
                if n == 0:
                    starts()
                    dve.sem_inc(pay_ready, 1)
                else:
                    dve.wait_ge(permuted, n)
                    V.tensor_copy(pay[0:EP, :, FRONT:FRONT + EC], perm_ps[0:EP, 0:NPAY * EC].rearrange("p (k c) -> p k c", k=NPAY))\
                        .then_inc(pay_ready, 1)
                dve.wait_ge(pay_ready, 2 * n + 1)
                if n < 2:
                    dve.wait_ge(rank_ready, 2 + n * (STEPS * UNIT + 1))
                    V.memset(onehot[:], 0.0).then_inc(pay_ready, 1)
                    dve.wait_ge(pay_ready, 2 * n + 2)

            def first():
                V.scalar_tensor_tensor(out=edge_f[0:EP, :], in0=pay[0:EP, 2, FRONT:FRONT + EC], scalar=float(EC),
                                       in1=pay[0:EP, 3, FRONT:FRONT + EC], op0=ALU.mult, op1=ALU.add)
                V.scalar_tensor_tensor(out=key[0:EP, 0:EC], in0=pay[0:EP, 0, FRONT:FRONT + EC], scalar=float(DIG),
                                       in1=pay[0:EP, 1, FRONT:FRONT + EC], op0=ALU.mult, op1=ALU.add).then_inc(key_ready, 1)
                dve.wait_ge(key_ready, 1)
                V.tensor_copy(key_i[0:EP, :], key[0:EP, 0:EC])
                V.tensor_copy(edge_i[0:EP, :], edge_f[0:EP, :])
                dve.wait_ge(key_mm, 2)
                V.tensor_copy(keyT[0:EC, :], perm_ps[0:EC, 0:EP]).then_inc(keyT_ready, 1)
                link(V.tensor_tensor(dup[0:EP, :], key[0:EP, 0:EC], rank_ps[0][0:EP, 0:EC], ALU.is_equal))
                link(V.scalar_tensor_tensor(out=target[0:EP, :], in0=dup[0:EP, :], scalar=SKIP, in1=key[0:EP, 0:EC],
                                            op0=ALU.mult, op1=ALU.add))
                V.tensor_copy(target_i[0:EP, :], target[0:EP, :]).then_inc(index_ready, 1)
                dve.wait_ge(keyB_loaded, 16)
                for part in sums(-1, 0):
                    part()

            def sums(g, r):
                def one(j):
                    def do():
                        c = J * (g + 1) + j
                        at_least(dve, same_free, c + 1, times(r, J))
                        V.tensor_scalar(same[0:EP, c % (2 * J), :], cut(keyB[0:EP, :], EP * c, times(r, J * EP), EP),
                                        cut(key[0:EP, :], c, times(r, J), 1), None, ALU.is_equal).then_inc(same_ready, 1)
                    return do
                return [one(j) for j in range(J)]

            def middle():
                dve.wait_ge(sum_ready, NE)
                last = sumT[:, :].rearrange("p (c e) -> p c e", e=EP)[:, :, EP - 1]
                V.tensor_copy(lastT[:], last).then_inc(last_ready, 1)
                dve.wait_ge(last_ready, 1)
                V.memset(last, 0.0)
                dve.wait_ge(last_mm, 1)
                V.tensor_copy(last_w[0:EC, :], perm_ps[0:EC, 0:P]).then_inc(last_w_ready, 1)

            def elu(c, m4, ps, bias, neg_bias, e, exp_ready, mn, min_ready, h, used, done):
                n = cols(c)
                at_least(dve, exp_ready, c + 1, m4)
                at_least(dve, done, c, m4)
                V.tensor_scalar(mn[:, 0:n], e[:, 0:n], 1.0, bias[:, 0:1], ALU.min, ALU.add).then_inc(min_ready, 1)
                at_least(dve, min_ready, c + 1, m4)
                at_least(dve, used, c - 1, m4)
                V.scalar_tensor_tensor(out=h[:, c % 2, 0:n], in0=ps[:, 0:n], scalar=neg_bias[:, 0:1],
                                       in1=mn[:, 0:n], op0=ALU.max, op1=ALU.add).then_inc(done, 1)

            def carries(c, m4, m):
                e = c - ND
                at_least(dve, l1_ready, c - 1, m4)
                if c == ND:
                    dve.wait_ge(last_w_ready, 1)
                V.tensor_scalar(carry[0:EC, c % 2, :], cut(keyB[0:EC, :], e * COLS, times(m, 4 * COLS), COLS),
                                keyT[0:EC, EP - 1:EP], None, ALU.is_equal).then_inc(carry_ready, 1)

            def normalise(c, m4, m):
                k = c % SLOTS
                q = rows(c)
                at_least(dve, rstd_ready, c + 1, m4)
                if not is_edge(c):
                    at_least(dve, stored[k], 16 * (c // SLOTS), times(m, 16))
                else:
                    if c - SLOTS < ND:
                        dve.wait_ge(stored[k], 16 * DENSE_ON[k])
                    at_least(dve, scattered[k], 64 * ((c - ND) // SLOTS), times(m, 64))
                V.tensor_tensor(o_sb[q, k, :].rearrange("p (j f) -> p j f", j=J),
                                z_ps[c % 2][q, :].rearrange("p (j f) -> p j f", j=J),
                                rstd[q, c % 2, :].rearrange("p (j a) -> p j a", a=1).to_broadcast([q.stop, J, P]),
                                ALU.mult).then_inc(o_ready, 1)

            def step(c, m4, m, beside):
                def first_layer():
                    if item_in(c) and is_edge(c):
                        carries(c, m4, m)
                    if item_in(c - 1):
                        elu(c - 1, m4, l1_ps, bias1, neg_bias1, e1, exp1_ready, m1, min1_ready, h1, l2_ready, h1_ready)

                def second_layer():
                    if item_in(c - 4):
                        normalise(c - 4, m4, m)
                    if item_in(c - 2):
                        elu(c - 2, m4, l2_ps, bias2, neg_bias2, e2, exp2_ready, m2, min2_ready, h2, z_ready, h2_ready)

                run([list, first_layer, second_layer], beside)

            constants()
            biases()
            digits()
            walk(dve, step, hist=hist, sort_batch=sort_batch, finish=finish, first=first, sums=sums, middle=middle)


_INS = ['x', 'src', 'edge_attr_128', 'L0_gnn_W0', 'L0_gnn_b0', 'L0_gnn_W2', 'L0_gnn_b2', 'L0_gnn_W3', 'L0_gnn_b3']


def kernel(**inputs):
    import numpy as _np
    import concourse.bacc as _bacc
    from concourse import mybir as _mybir
    from concourse.bass_utils import run_bass_kernel_spmd as _run

    nc = _bacc.Bacc("TRN2", target_bir_lowering=False, num_devices=1)
    arrays, args = {}, []
    for name in _INS:
        a = _np.ascontiguousarray(inputs[name])
        arrays[f"in_{name}_dram"] = a
        args.append(nc.dram_tensor(f"in_{name}_dram", a.shape, _mybir.dt.from_np(a.dtype), kind="ExternalInput").ap())
    key_rows = nc.dram_tensor("key_rows_dram", inputs['src'].shape, _mybir.dt.float32, kind="Internal").ap()
    out = nc.dram_tensor("out_0_dram", inputs['x'].shape, _mybir.dt.float32, kind="ExternalOutput").ap()
    x_rows = nc.dram_tensor('x_rows_dram', (inputs['src'].shape[0] // J, J * inputs['x'].shape[1]), _mybir.dt.float32, kind='Internal').ap()
    gnn_resnorm(nc, *args, key_rows, x_rows, out)
    r = _run(nc, [arrays], core_ids=[0])
    return r.results[0]["out_0_dram"]
```

```python
from contextlib import ExitStack

import concourse.bass as bass
from concourse import mybir

ALU = mybir.AluOpType
ACT = mybir.ActivationFunctionType
AX_X = mybir.AxisListType.X
F32 = mybir.dt.float32
BF16 = mybir.dt.bfloat16
I32 = mybir.dt.int32

P = 128
J = 4
EP = 125
DIG = 256
UNIT = 5
NPAY = 4
EPS = 1e-5
ROUND = 12582912.0
SKIP = 65536.0


def gnn_resnorm(nc, x, src, attr, W0, b0, W2, b2, W3, b3, key_rows, x_rows, out):
    N, F = x.shape
    E = src.shape[0]
    assert F == P and E % (EP * J) == 0 and N < DIG * DIG and N < SKIP
    EC = E // EP
    ROWS = J * P
    COLS = J * EP
    ND = -(-N // ROWS)
    NE = EC // J
    NI = ND + NE
    SLOTS = 4
    PASS = EC // UNIT
    LAG = 4
    STEPS = PASS + LAG

    HEAD = 2
    AT_PASS = (HEAD, HEAD + STEPS)
    AT_KEYS = HEAD + 2 * STEPS
    AT_SUMS = AT_KEYS + 4
    AT_GATHER = AT_SUMS + NE - 1
    KEY_PARTS = 5
    AHEAD = 2
    LOOP_GATHER = (ND - 1 - AHEAD - AT_GATHER) // 4
    MID = AT_GATHER + 4 * LOOP_GATHER
    GATHER_END = AT_GATHER + NE - 1
    AT_EDGES = -(-(ND + 5) // 4) * 4
    LOOP_EDGES = (NI - AHEAD - AT_EDGES) // 4
    STEPS_END = NI + 5
    HALF = 16
    BLOCK = P // HALF
    BLOCKS = -(-EC // BLOCK)
    assert PASS % 4 == 0 and LAG == 4 and (NE - 1) % 4 == 0 and EC % UNIT == 0 and HALF * HALF == DIG
    assert MID <= GATHER_END <= AT_EDGES and GATHER_END - NE + 1 + AHEAD < ND

    with ExitStack() as ctx:
        def sb(name, shape, dt=F32):
            return ctx.enter_context(nc.sbuf_tensor(name, shape, dt))

        def psum(name):
            return ctx.enter_context(nc.psum_tensor(name, [P, J * P], F32))

        def sem(name):
            return ctx.enter_context(nc.semaphore(name))

        xT_ps = psum("xT_ps")
        l1_ps = psum("l1_ps")
        l2_ps = psum("l2_ps")
        z_ps = [psum(f"z_ps{k}") for k in range(2)]
        rank_ps = [psum(f"rank_ps{k}") for k in range(2)]
        perm_ps = psum("perm_ps")

        w0x = sb("w0x", [P, P])
        w0e = sb("w0e", [P, P])
        w2 = sb("w2", [P, P])
        w3 = sb("w3", [P, P])
        w3c = sb("w3c", [P, P])
        b_in = sb("b_in", [P, 3])
        w3_sum = sb("w3_sum", [P, 1])
        w3_mean = sb("w3_mean", [P, 1])
        minus_one = sb("minus_one", [P, 1])
        bias_x = sb("bias_x", [P, 1])
        bias1 = sb("bias1", [P, 1])
        neg_bias1 = sb("neg_bias1", [P, 1])
        bias2 = sb("bias2", [P, 1])
        neg_bias2 = sb("neg_bias2", [P, 1])
        bias_rest = sb("bias_rest", [P, 2])
        bias_low = sb("bias_low", [P, 2], BF16)
        bias_parts = sb("bias_parts", [P, 2, 3])
        bias_rows = sb("bias_rows", [P, 2, P], BF16)
        ones_row = sb("ones_row", [P, J * P], BF16)
        eps = sb("eps", [P, 1])
        neg_half = sb("neg_half", [P, J])
        diff_i = sb("diff_i", [P, P], I32)
        diff = sb("diff", [P, P])
        count_i = sb("count_i", [P, DIG], I32)
        count = sb("count", [P, DIG], BF16)
        prow_i = sb("prow_i", [P, 1], I32)
        ident = sb("ident", [P, P])
        center = sb("center", [P, P])
        before = sb("before", [P, P], BF16)
        not_before = sb("not_before", [P, P], BF16)
        ones = sb("ones", [P, P], BF16)
        next_row = sb("next_row", [P, P])
        next_col = sb("next_col", [P, P])
        zeros = sb("zeros", [P, DIG])
        zeros_b = sb("zeros_b", [P, J * P], BF16)

        with ExitStack() as sorting:
            def sb_sort(name, shape, dt=F32):
                return sorting.enter_context(nc.sbuf_tensor(name, shape, dt))

            nibble_i = sb_sort("nibble_i", [P, 2, 2, EC], I32)
            nibble = sb_sort("nibble", [P, 2, 2, EC], BF16)
            nibble_hot = sb_sort("nibble_hot", [P, 2, 2, BLOCKS * P], BF16)
            row_hot = sb_sort("row_hot", [P, 4 * UNIT, EP], BF16)
            col_hot = sb_sort("col_hot", [P, 4 * UNIT, EC], BF16)
            col_pay = sb_sort("col_pay", [P, 2 * UNIT, NPAY, EC], BF16)
            block_sum = sb_sort("block_sum", [P, 2, P])
            totals = sb_sort("totals", [P, 2, DIG])
            start = sb_sort("start", [P, 2, DIG])
            start_i = sb_sort("start_i", [P, 3, 2, DIG], I32)
            digit_sum = sb_sort("digit_sum", [P, 2, DIG])
            onehot = sb_sort("onehot", [P, 2 * UNIT, DIG], BF16)
        sumT = sb("sumT", [P, E])

        src_i = sb("src_i", [P, EC], I32)
        digit_i = sb("digit_i", [P, 2, EC], I32)
        pay = sb("pay", [P, NPAY, EC])
        pay_last = sb("pay_last", [P, 2, UNIT])
        count_half_i = sb("count_half_i", [P, DIG], I32)
        count_half = sb("count_half", [P, DIG])
        prow_half_i = sb("prow_half_i", [P, 2], I32)
        prow_half = sb("prow_half", [P, 2])
        same_block = sb("same_block", [P, P])
        same_half = sb("same_half", [P, DIG])
        ones_f = sb("ones_f", [P, P])
        half_sum = sb("half_sum", [P, 2, HALF])
        start_b = sb("start_b", [P, 2, 2, DIG], BF16)
        picked = sb("picked", [P, 2, DIG])
        pos = sb("pos", [P, EC])
        quot = sb("quot", [P, EC])
        pos_col = sb("pos_col", [P, EC])
        pos_row = sb("pos_row", [P, EC])

        key = sb("key", [P, EC + 1])
        key_i = sb("key_i", [P, EC], I32)
        edge_f = sb("edge_f", [P, EC])
        edge_i = sb("edge_i", [P, EC], I32)
        dup = sb("dup", [P, EC])
        target = sb("target", [P, EC])
        target_i = sb("target_i", [P, EC], I32)
        keyT = sb("keyT", [P, EP])
        keyB = sb("keyB", [P, E])
        attr_sb = sb("attr_sb", [P, SLOTS, J, P])
        same = sb("same", [P, 2 * J, EP])
        lastT = sb("lastT", [P, EC])
        last_sum = sb("last_sum", [P, P])
        carry_mask = sb("carry_mask", [P, 2, COLS])
        attr_idx = sb("attr_idx", [P, SLOTS, J], I32)
        x_idx = sb("x_idx", [P, SLOTS, J], I32)
        out_idx = sb("out_idx", [P, SLOTS, J], I32)
        xg_sb = sb("xg_sb", [P, SLOTS, J * P])

        x_sb = sb("x_sb", [P, SLOTS, J * P])
        xT = sb("xT", [P, SLOTS, J * P])
        e1 = sb("e1", [P, 2, J * P])
        e2 = sb("e2", [P, 2, J * P])
        m1 = sb("m1", [P, 2, J * P])
        m2 = sb("m2", [P, 2, J * P])
        h1 = sb("h1", [P, 2, J * P])
        h2 = sb("h2", [P, 2, J * P])
        sq = sb("sq", [P, J, P])
        ssq = sb("ssq", [P, 2, J])
        var_eps = sb("var_eps", [P, 2, J])
        rstd = sb("rstd", [P, 2, J])
        o_sb = sb("o_sb", [P, SLOTS, J * P])

        weights_loaded = sem("weights_loaded")
        src_loaded = sem("src_loaded")
        consts_made = sem("consts_made")
        dve_chain = sem("dve_chain")
        pool_waits = sem("pool_waits")
        sp_waits = sem("sp_waits")
        setup_mm = sem("setup_mm")
        b3_ready = sem("b3_ready")
        biases_ready = sem("biases_ready")
        onehot_ready = sem("onehot_ready")
        tables_cleared = sem("tables_cleared")
        nibbles_ready = sem("nibbles_ready")
        blocks_counted = sem("blocks_counted")
        digits_folded = sem("digits_folded")
        hist_done = sem("hist_done")
        start_ready = sem("start_ready")
        rank_ready = sem("rank_ready")
        rank_free = sem("rank_free")
        place_known = sem("place_known")
        col_ready = sem("col_ready")
        pay_act = sem("pay_act")
        pay_pool = sem("pay_pool")
        pay_last_ready = sem("pay_last_ready")
        place_free = sem("place_free")
        permuted = sem("permuted")
        pay_ready = sem("pay_ready")
        key_ready = sem("key_ready")
        key_mm = sem("key_mm")
        keyT_ready = sem("keyT_ready")
        keys_stored = sem("keys_stored")
        keyB_loaded = sem("keyB_loaded")
        index_ready = sem("index_ready")
        attr_idx_ready = sem("attr_idx_ready")
        attr_loaded = [sem(f"attr_loaded{k}") for k in range(SLOTS)]
        same_ready = sem("same_ready")
        same_free = sem("same_free")
        sum_ready = sem("sum_ready")
        last_ready = sem("last_ready")
        last_turned = sem("last_turned")
        last_sum_ready = sem("last_sum_ready")
        carry_ready = sem("carry_ready")
        carry_mm = sem("carry_mm")
        carried = sem("carried")

        x_loaded = [sem(f"x_loaded{k}") for k in range(SLOTS)]
        x_gathered = [sem(f"x_gathered{k}") for k in range(SLOTS)]
        x_stashed = [sem(f"x_stashed{k}") for k in range(SLOTS)]
        x_idx_ready = sem("x_idx_ready")
        xT_ps_ready = sem("xT_ps_ready")
        xT_ready = sem("xT_ready")
        l1_ready = sem("l1_ready")
        exp1_ready = sem("exp1_ready")
        min1_ready = sem("min1_ready")
        h1_ready = sem("h1_ready")
        l2_ready = sem("l2_ready")
        exp2_ready = sem("exp2_ready")
        min2_ready = sem("min2_ready")
        h2_ready = sem("h2_ready")
        z_ready = sem("z_ready")
        ssq_ready = sem("ssq_ready")
        var_ready = sem("var_ready")
        var_by_pool = sem("var_by_pool")
        rstd_ready = sem("rstd_ready")
        o_ready = sem("o_ready")
        stored = [sem(f"stored{k}") for k in range(SLOTS)]
        scattered = [sem(f"scattered{k}") for k in range(SLOTS)]

        DENSE_ON = [len(range(k, ND, SLOTS)) for k in range(SLOTS)]

        def at_least(eng, semaphore, const, reg=0):
            if isinstance(reg, int):
                if const + reg > 0:
                    eng.wait_ge(semaphore, const + reg)
            else:
                assert const >= 0, const
                eng.wait_ge(semaphore, reg + const)

        def carried_at_least(eng, carrier, semaphore, const, reg=0):
            at_least(eng, semaphore, const, reg)
            if not isinstance(reg, int):
                eng.sem_inc(carrier, 1)

        def cut(ap, const, reg, size):
            if isinstance(reg, int):
                return ap[:, const + reg:const + reg + size]
            return ap[:, bass.ds(reg + const, size)]

        def columns(const, reg, size):
            return slice(const + reg, const + reg + size) if isinstance(reg, int) else bass.ds(reg + const, size)

        def act_payloads(u):
            return NPAY - 2 if u % 2 == 0 else NPAY - 1

        def times(reg, k):
            return reg * k

        def in_pass(batch):
            return 0 <= batch < PASS

        def items_in_sort(k):
            return 2 * STEPS - max(0, k - HEAD)

        def in_sort(s):
            return AT_PASS[0] <= s < AT_KEYS

        def is_edge(c):
            return c >= ND

        def item_in(c):
            return 0 <= c < NI

        def cols(c):
            return COLS if is_edge(c) else ROWS

        def rows(c):
            return slice(0, EP if is_edge(c) else P)

        def none(*_):
            return []

        def walk(eng, step, hist=none, sort_batch=none, finish=none, first=none, keys=none, before_sums=none, sums=none, middle=none,
                 gather=none, after_gather=none, last=none):
            for c in range(HEAD):
                step(c, 0, 0, hist(c))
            for n in range(2):
                finish(n)
                for t in range(LAG):
                    step(AT_PASS[n] + t, 0, 0, sort_batch(n, t, 0))
                with eng.Fori(0, (PASS - LAG) // 4) as m:
                    for u in range(4):
                        t = LAG + u
                        step(AT_PASS[n] + t, m * 4, m, sort_batch(n, t, m * 4))
                for t in range(PASS, STEPS):
                    step(AT_PASS[n] + t, 0, 0, sort_batch(n, t, 0))
            finish(2)
            first()
            for c in range(AT_KEYS, AT_SUMS):
                step(c, 0, 0, keys(c - AT_KEYS))
            before_sums()
            with eng.Fori(0, (NE - 1) // 4 - 1) as m:
                for u in range(4):
                    step(AT_SUMS + u, m * 4, m, sums(u, m * 4))
            for g in range(NE - 5, NE - 1):
                step(AT_SUMS + g, 0, 0, sums(g, 0))
            middle()
            with eng.Fori(0, LOOP_GATHER) as m:
                for u in range(4):
                    step(AT_GATHER + u, m * 4, m, gather(u, m * 4))
            for c in range(MID, AT_EDGES):
                if c == GATHER_END:
                    after_gather()
                if c == ND + 5:
                    last()
                step(c, 0, 0, gather(c - AT_GATHER, 0) if c < GATHER_END else [])
            if GATHER_END == AT_EDGES:
                after_gather()
            if AT_EDGES == ND + 5:
                last()
            with eng.Fori(0, LOOP_EDGES) as m:
                for u in range(4):
                    step(AT_EDGES + u, m * 4, m, [])
            for c in range(AT_EDGES + 4 * LOOP_EDGES, STEPS_END):
                step(c, 0, 0, [])

        def run(parts, beside):
            beside = list(beside)
            for part in parts:
                part()
                if beside:
                    beside.pop(0)()
            for part in beside:
                part()

        block = ctx.enter_context(nc.Block())

        @block.sync
        def _(sp):
            sp.dma_start(src_i[0:EP, :], src.rearrange("(p c) -> p c", p=EP)).then_inc(src_loaded, 16)
            sp.dma_start(w0x[:], W0[0:P, :]).then_inc(weights_loaded, 16)
            sp.dma_start(w0e[:], W0[P:2 * P, :]).then_inc(weights_loaded, 16)
            sp.dma_start(w2[:], W2[:, :]).then_inc(weights_loaded, 16)
            sp.dma_start(w3[:], W3[:, :]).then_inc(weights_loaded, 16)
            for k, b in enumerate((b0, b2, b3)):
                sp.dma_start(b_in[:, k:k + 1], b.rearrange("(p a) -> p a", a=1)).then_inc(weights_loaded, 16)

            def rows_of(ap, c, m):
                if c == ND - 1:
                    part = ap[N - ROWS:N, :]
                elif isinstance(m, int):
                    part = ap[c * ROWS:(c + 1) * ROWS, :]
                else:
                    part = ap[bass.ds(m * (4 * ROWS) + c * ROWS, ROWS), :]
                return part.rearrange("(p j) f -> p (j f)", p=P)

            def x_rows_of(e, r):
                part = x_rows[bass.ds(r * EP + e * EP, EP), :] if not isinstance(r, int) else x_rows[e * EP:(e + 1) * EP, :]
                return part

            def stash(e, r):
                carried_at_least(sp, sp_waits, x_gathered[e % SLOTS], 64 * (e // SLOTS + 1), times(r, 64 // SLOTS))
                sp.dma_start(x_rows_of(e, r), xg_sb[0:EP, e % SLOTS, :]).then_inc(x_stashed[e % SLOTS], 16)

            def load(c, m4, m):
                k = c % SLOTS
                if not item_in(c):
                    return
                carried_at_least(sp, sp_waits, xT_ps_ready, c - SLOTS + 1, m4)
                if not is_edge(c):
                    sp.dma_start(x_sb[:, k, :], rows_of(x, c, m)).then_inc(x_loaded[k], 16)
                else:
                    e = c - ND
                    carried_at_least(sp, sp_waits, x_stashed[e % SLOTS], 16 * (e // SLOTS + 1), times(m, 16))
                    sp.dma_start(x_sb[0:EP, k, :], x_rows_of(e, m4)).then_inc(x_loaded[k], 16)

            def step(c, m4, m, beside):
                load(c + AHEAD, m4, m)
                i = c - 4
                if 0 <= i < ND:
                    carried_at_least(sp, sp_waits, o_ready, i + 1, m4)
                    if i == ND - 1:
                        sp.wait_ge(stored[(i - 1) % SLOTS], 16 * DENSE_ON[(i - 1) % SLOTS])
                    sp.dma_start(rows_of(out, i, m), o_sb[:, i % SLOTS, :]).then_inc(stored[i % SLOTS], 16)
                for part in beside:
                    part()

            for c in range(AHEAD):
                load(c, 0, 0)
            def first():
                sp.wait_ge(keyT_ready, 1)
                sp.dma_start(key_rows.rearrange("(c e) -> c e", e=EP), keyT[0:EC, :]).then_inc(keys_stored, 16)
                sp.wait_ge(keys_stored, 16)
                load_keys(0)

            def load_keys(part):
                size = E // KEY_PARTS
                sp.dma_start(keyB[:, part * size:(part + 1) * size],
                             key_rows[part * size:(part + 1) * size].rearrange("(a e) -> a e", a=1).to_broadcast([P, size]))\
                    .then_inc(keyB_loaded, 16)

            def keys(c):
                return [lambda: load_keys(c + 1)]

            walk(sp, step, first=first, keys=keys, gather=lambda e, r: [lambda: stash(e, r)], after_gather=lambda: stash(NE - 1, 0))
            for k in range(SLOTS):
                sp.wait_ge(stored[k], 16 * DENSE_ON[k])

        @block.gpsimd
        def _(pool):
            nc.gpsimd.iota(diff_i[:], pattern=[[1, P]], base=0, channel_multiplier=-1).then_inc(consts_made, 1)
            nc.gpsimd.iota(count_i[:], pattern=[[1, DIG]], base=0, channel_multiplier=0).then_inc(consts_made, 1)
            nc.gpsimd.iota(prow_i[:], pattern=[[0, 1]], base=0, channel_multiplier=1).then_inc(consts_made, 1)
            nc.gpsimd.memset(nibble_hot[:], 0.0).then_inc(tables_cleared, 1)
            pool.wait_ge(biases_ready, 1)

            def sort_batch(n, t, r):
                b = t - 3
                if not in_pass(b):
                    return []

                def one(u):
                    def do():
                        c = UNIT * b + u
                        done = n * EC + c
                        if u == 0:
                            carried_at_least(pool, pool_waits, pay_pool, done, times(r, UNIT))
                            nc.gpsimd.tensor_copy(pay_last[0:EP, :, :], pay[0:EP, NPAY - 2:NPAY, columns(c, times(r, UNIT), UNIT)])\
                                .then_inc(pay_last_ready, 1)
                            carried_at_least(pool, pool_waits, pay_last_ready, n * PASS + b + 1, r)
                        carried_at_least(pool, pool_waits, col_ready, done + 1, times(r, UNIT))
                        carried_at_least(pool, pool_waits, place_free, done + 1, times(r, UNIT))
                        for k in range(act_payloads(u), NPAY):
                            paid = nc.gpsimd.tensor_scalar(col_pay[0:EP, UNIT * (b % 2) + u, k, :],
                                                           col_hot[0:EP, UNIT * (b % 4) + u, :],
                                                           pay_last[0:EP, k - (NPAY - 2), u:u + 1], None, ALU.mult)
                        paid.then_inc(pay_pool, 1)
                    return do
                return [one(u) for u in range(UNIT)]

            def gather_attr(g, r):
                gp = g % SLOTS
                carried_at_least(pool, pool_waits, same_free, 2 * J + J * (g - SLOTS + 1), times(r, J))
                carried_at_least(pool, pool_waits, attr_idx_ready, g + 1, r)
                for j in range(J):
                    nc.gpsimd.indirect_dma_start(
                        out=attr_sb[0:EP, gp, j, :], out_offset=None, in_=attr[:, :],
                        in_offset=bass.IndirectOffsetOnAxis(ap=attr_idx[0:EP, gp, j:j + 1], axis=0),
                    ).then_inc(attr_loaded[gp], 16)

            def gather_x(e, r):
                gp = e % SLOTS
                carried_at_least(pool, pool_waits, x_stashed[gp], 16 * (e // SLOTS), times(r, 16 // SLOTS))
                carried_at_least(pool, pool_waits, x_idx_ready, e + 1, r)
                for j in range(J):
                    nc.gpsimd.indirect_dma_start(
                        out=xg_sb[0:EP, e % SLOTS, j * P:(j + 1) * P], out_offset=None, in_=x[:, :],
                        in_offset=bass.IndirectOffsetOnAxis(ap=x_idx[0:EP, e % SLOTS, j:j + 1], axis=0),
                    ).then_inc(x_gathered[gp], 16)

            def scatter_out(c, m4, m):
                k = c % SLOTS
                e = c - ND
                carried_at_least(pool, pool_waits, o_ready, c + 1, m4)
                for j in range(J):
                    nc.gpsimd.indirect_dma_start(
                        out=out[:, :], out_offset=bass.IndirectOffsetOnAxis(ap=out_idx[0:EP, k, j:j + 1], axis=0),
                        in_=o_sb[0:EP, k, j * P:(j + 1) * P], in_offset=None,
                        bounds_check=N - 1, oob_is_err=False,
                    ).then_inc(scattered[k], 16)

            def step(c, m4, m, beside):
                for part in beside:
                    part()
                if item_in(c - 5) and is_edge(c - 5):
                    scatter_out(c - 5, m4, m)
                if item_in(c - 3):
                    i = c - 3
                    q = rows(i)
                    if in_sort(c):
                        carried_at_least(pool, pool_waits, ssq_ready, i + 1, m4)
                        nc.gpsimd.tensor_scalar(var_eps[q, i % 2, :], ssq[q, i % 2, :], EPS, None, ALU.add).then_inc(var_by_pool, 1)
                        at_least(pool, var_by_pool, i + 1 - max(0, HEAD - 3), m4)
                    else:
                        at_least(pool, var_ready, i + 1 - (items_in_sort(3) if c >= AT_KEYS else 0), m4)
                    carried_at_least(pool, pool_waits, o_ready, i - 1, m4)
                    nc.gpsimd.tensor_tensor(rstd[q, i % 2, :], var_eps[q, i % 2, :], neg_half[q, :], ALU.pow)\
                        .then_inc(rstd_ready, 1)

            def finish(n):
                if n < 2:
                    pool.wait_ge(pay_ready, n + 1)

            def keys(c):
                return [lambda: gather_attr(c, 0) if c < SLOTS - 1 else gather_x(0, 0)]

            def last():
                for k in range(SLOTS):
                    pool.wait_ge(stored[k], 16 * DENSE_ON[k])

            walk(pool, step, finish=finish, keys=keys, last=last,
                 sort_batch=sort_batch,
                 sums=lambda g, r: [lambda: gather_attr(g + 3, r) if g + 3 < NE else gather_x(g + 4 - NE, 0)],
                 gather=lambda e, r: [lambda: gather_x(e + 3, r)] if e + 3 < NE else [])
            for k in range(SLOTS):
                pool.wait_ge(scattered[k], 64 * len([i for i in range(ND, NI) if i % SLOTS == k]))

        @block.tensor
        def _(pe):
            T = nc.tensor

            def count_blocks():
                for n in range(2):
                    pe.wait_ge(nibbles_ready, 2 * n + 2)
                    for g in range(BLOCKS):
                        mm = T.matmul(rank_ps[n][:, 0:P], nibble_hot[0:EP, n, 0, g * P:(g + 1) * P],
                                      nibble_hot[0:EP, n, 1, g * P:(g + 1) * P], start=(g == 0), stop=(g == BLOCKS - 1))
                    mm.then_inc(blocks_counted, 1)

            def small_products():
                pe.sem_inc(place_free, 2 * UNIT)
                pe.sem_inc(same_free, 2 * J)
                pe.sem_inc(sum_ready, 2)
                pe.sem_inc(carry_mm, 1)
                pe.sem_inc(carried, 2)
                pe.wait_ge(weights_loaded, 16 * 7)
                pe.wait_ge(b3_ready, 1)
                T.matmul(l1_ps[:, 0:1], w2[:], minus_one[:], start=True, stop=True)
                T.matmul(l2_ps[:, 0:1], center[:], b_in[:, 2:3], start=True, stop=False)
                T.matmul(l2_ps[:, 0:1], w3c[:], minus_one[:], start=False, stop=True).then_inc(setup_mm, 1)
                pe.wait_ge(b3_ready, 2)
                T.matmul(z_ps[0][:, 0:1], w0x[:], bias_x[:], start=True, stop=True).then_inc(setup_mm, 1)
                pe.wait_ge(biases_ready, 1)
                for k in range(2):
                    mm = T.transpose(z_ps[k][0:3, 0:P], bias_parts[:, k, :], ident[:])
                mm.then_inc(setup_mm, 1)
                pe.wait_ge(biases_ready, 2)

            def clear(bank, first):
                return T.matmul(bank[0:EP, :], ones[0:EP, 0:EP], zeros_b[0:EP, :], start=first, stop=not first,
                                skip_group_check=True)

            def hist(c):
                def total(n):
                    pe.wait_ge(digits_folded, n + 1)
                    T.matmul(rank_ps[n][0:EP, 0:DIG], ones_f[:, 0:EP], digit_sum[:, n, :], start=True, stop=True)\
                        .then_inc(hist_done, 1)

                return [count_blocks, lambda: (total(0), total(1))] if c == 0 else []

            def sort_batch(n, t, r):
                reg = times(r, UNIT)

                def rank(u):
                    c = UNIT * (t - 1) + u
                    bank = rank_ps[c % 2][0:EP, 0:DIG]
                    at_least(pe, onehot_ready, n * EC + c + 1, reg)
                    at_least(pe, rank_free, n * EC + c, reg)
                    for weights, back in ((not_before, 2), (ones, 1), (before, 0)):
                        if c >= back:
                            mm = T.matmul(bank, weights[0:EP, 0:EP], onehot[0:EP, (c - back) % (2 * UNIT), :],
                                          start=False, stop=False, skip_group_check=True)
                    mm.then_inc(rank_ready, 1)

                def place(u):
                    b = t - 4
                    done = n * EC + UNIT * b + u
                    at_least(pe, pay_act, done + 1, reg)
                    at_least(pe, pay_pool, done + 1, reg)
                    T.matmul(perm_ps[0:EP, 0:NPAY * EC], row_hot[0:EP, UNIT * (b % 4) + u, :],
                             col_pay[0:EP, UNIT * (b % 2) + u, :, :].rearrange("p k c -> p (k c)"),
                             start=False, stop=False, skip_group_check=True).then_inc(place_free, 1)

                def piece(u):
                    if in_pass(t - 4):
                        place(u)
                    if in_pass(t - 1):
                        rank(u)

                return [lambda u=u: piece(u) for u in range(UNIT)]

            def finish(n):
                if n > 0:
                    clear(perm_ps, False).then_inc(permuted, 1)
                if n < 2:
                    pe.wait_ge(start_ready, 1)
                    pe.wait_ge(rank_free, n * EC + 1)
                    for bank in rank_ps:
                        for part in range(2):
                            mm = T.matmul(bank[0:EP, 0:DIG], ones[0:1, 0:EP], start_b[0:1, part, n, :],
                                          start=(part == 0), stop=False, skip_group_check=True)
                    mm.then_inc(rank_ready, 1)
                    pe.wait_ge(pay_ready, n + 1)
                    clear(perm_ps, True)

            def first():
                pe.wait_ge(key_ready, 1)
                T.matmul(rank_ps[0][0:EP, 0:EC], next_row[0:EP, 0:EP], key[0:EP, 0:EC], start=True, stop=False)
                T.matmul(rank_ps[0][0:EP, 0:EC], next_col[0:EP, 0:EP], key[0:EP, 1:EC + 1],
                         start=False, stop=True).then_inc(key_mm, 1)
                T.transpose(perm_ps[0:EC, 0:EP], key[0:EP, 0:EC], ident[0:EP, 0:EP]).then_inc(key_mm, 1)
                pe.wait_ge(index_ready, 1)

            def sums(g, r):
                def one(j):
                    def do():
                        if j == 0:
                            at_least(pe, attr_loaded[g % SLOTS], 64 * (g // SLOTS + 1), times(r, 64 // SLOTS))
                            at_least(pe, sum_ready, g + 1, r)
                        at_least(pe, same_ready, J * g + j + 1, times(r, J))
                        T.matmul(rank_ps[g % 2][:, j * EP:(j + 1) * EP], attr_sb[0:EP, g % SLOTS, j, :],
                                 same[0:EP, J * (g % 2) + j, :],
                                 start=(j == 0), stop=(j == J - 1), skip_group_check=True).then_inc(same_free, 1)
                    return do
                return [one(j) for j in range(J)]

            def middle():
                for part in sums(NE - 1, 0):
                    part()
                pe.wait_ge(last_ready, 1)
                T.transpose(perm_ps[0:EC, 0:P], lastT[:], ident[:]).then_inc(last_turned, 1)
                pe.wait_ge(last_sum_ready, 1)

            def carry(e, r):
                def do():
                    at_least(pe, carry_ready, e + 1, r)
                    at_least(pe, carried, e + 1, r)
                    T.matmul(rank_ps[e % 2][:, 0:COLS], last_sum[0:EC, :], carry_mask[0:EC, e % 2, :],
                             start=True, stop=True).then_inc(carry_mm, 1)
                return [do]

            def add_bias(ps, k, n, done):
                T.matmul(ps, bias_rows[0:3, k, :], ones_row[0:3, 0:n], start=False, stop=True).then_inc(done, 1)

            def layer1(c, m4, m):
                n = cols(c)
                at_least(pe, xT_ready, c + 1, m4)
                at_least(pe, h1_ready, c, m4)
                ps = l1_ps[:, 0:n]
                if in_sort(c + 1):
                    T.matmul(ps, w0x[:], xT[:, c % SLOTS, 0:n], start=True, stop=False)
                    add_bias(ps, 0, n, l1_ready)
                    return
                if not is_edge(c):
                    T.matmul(ps, w0x[:], xT[:, c % SLOTS, 0:n], start=True, stop=True).then_inc(l1_ready, 1)
                    return
                e = c - ND
                T.matmul(ps, w0x[:], xT[:, c % SLOTS, 0:n], start=True, stop=False)
                at_least(pe, carried, e + 3, m4)
                T.matmul(ps, w0e[:], cut(sumT[:, :], e * COLS, times(m, 4 * COLS), COLS), start=False, stop=True)\
                    .then_inc(l1_ready, 1)

            def turn(c, m4, m):
                q = EP if is_edge(c) else P
                at_least(pe, x_loaded[c % SLOTS], 16 * (c // SLOTS + 1), times(m, 16))
                at_least(pe, xT_ready, c, m4)
                for j in range(J):
                    mm = T.transpose(xT_ps[:, j * q:(j + 1) * q], x_sb[0:q, c % SLOTS, j * P:(j + 1) * P],
                                     ident[0:q, 0:q])
                mm.then_inc(xT_ps_ready, 1)

            def layer2(c, m4):
                n = cols(c)
                at_least(pe, h1_ready, c + 1, m4)
                at_least(pe, h2_ready, c, m4)
                if in_sort(c + 2):
                    T.matmul(l2_ps[:, 0:n], w2[:], h1[:, c % 2, 0:n], start=True, stop=False)
                    add_bias(l2_ps[:, 0:n], 1, n, l2_ready)
                else:
                    T.matmul(l2_ps[:, 0:n], w2[:], h1[:, c % 2, 0:n], start=True, stop=True).then_inc(l2_ready, 1)

            def layer3(c, m4):
                q = EP if is_edge(c) else P
                at_least(pe, h2_ready, c + 1, m4)
                at_least(pe, o_ready, c - 1, m4)
                for j in range(J):
                    z = z_ps[c % 2][0:q, j * P:(j + 1) * P]
                    T.matmul(z, xT[:, c % SLOTS, j * q:(j + 1) * q], center[:], start=True, stop=False)
                    mm = T.matmul(z, h2[:, c % 2, j * q:(j + 1) * q], w3c[:], start=False, stop=True)
                mm.then_inc(z_ready, 1)

            def step(c, m4, m, beside):
                parts = []
                if item_in(c - 1):
                    parts.append(lambda: layer1(c - 1, m4, m))
                if item_in(c):
                    parts.append(lambda: turn(c, m4, m))
                if item_in(c - 2):
                    parts.append(lambda: layer2(c - 2, m4))
                if item_in(c - 3):
                    parts.append(lambda: layer3(c - 3, m4))
                run(parts, beside)

            small_products()
            walk(pe, step, hist=hist, sort_batch=sort_batch, finish=finish, first=first, sums=sums, middle=middle,
                 gather=carry, after_gather=lambda: carry(NE - 1, 0)[0]())

        @block.scalar
        def _(act):
            A = nc.scalar

            def sort_batch(n, t, r):
                b = t - 3
                if not in_pass(b):
                    return []

                def one(u):
                    def do():
                        c = UNIT * b + u
                        at_least(act, col_ready, n * EC + c + 1, times(r, UNIT))
                        at_least(act, place_free, n * EC + c + 1, times(r, UNIT))
                        for k in range(act_payloads(u)):
                            paid = A.activation(col_pay[0:EP, UNIT * (b % 2) + u, k, :],
                                                col_hot[0:EP, UNIT * (b % 4) + u, :], ACT.Copy,
                                                scale=cut(pay[0:EP, k, :], c, times(r, UNIT), 1))
                        paid.then_inc(pay_act, 1)
                    return do
                return [one(u) for u in range(UNIT)]

            def finish(n):
                if n < 2:
                    act.wait_ge(pay_ready, n + 1)

            def copy_sums(g, r):
                def do():
                    at_least(act, same_free, 2 * J + J * (g + 1), times(r, J))
                    A.copy(cut(sumT[:, :], COLS * g, times(r, COLS), COLS), rank_ps[g % 2][:, 0:COLS]).then_inc(sum_ready, 1)
                return [list] * (J + 1) + [do]

            def turned(c, m4):
                n = cols(c)
                at_least(act, xT_ps_ready, c + 1, m4)
                at_least(act, z_ready, c - SLOTS + 1, m4)
                A.activation(xT[:, c % SLOTS, 0:n], xT_ps[:, 0:n], ACT.Identity, bias=bias_x[:, 0:1]).then_inc(xT_ready, 1)

            def exp(c, m4, ps, ready, bias, e, free, done):
                n = cols(c)
                at_least(act, ready, c + 1, m4)
                at_least(act, free, c - 1, m4)
                A.activation(e[:, c % 2, 0:n], ps[:, 0:n], ACT.Exp, bias=bias[:, 0:1]).then_inc(done, 1)

            def squares(c, m4):
                q = rows(c)
                at_least(act, z_ready, c + 1, m4)
                at_least(act, rstd_ready, c - 1, m4)
                at_least(act, ssq_ready, c, m4)
                for j in range(J):
                    t = A.activation(sq[q, j, :], z_ps[c % 2][q, j * P:(j + 1) * P], ACT.Square,
                                     scale=float(P) ** -0.5, accum_out=ssq[q, c % 2, j:j + 1])
                t.then_inc(ssq_ready, 1)

            def variance(c, m4):
                q = rows(c)
                at_least(act, ssq_ready, c + 1, m4)
                A.activation(var_eps[q, c % 2, :], ssq[q, c % 2, :], ACT.Identity, bias=eps[q, 0:1]).then_inc(var_ready, 1)

            def step(c, m4, m, beside):
                parts = []
                if item_in(c - 1):
                    parts.append(lambda: exp(c - 1, m4, l1_ps, l1_ready, minus_one if in_sort(c) else bias1, e1,
                                             h1_ready, exp1_ready))
                if item_in(c):
                    parts.append(lambda: turned(c, m4))
                if item_in(c - 2):
                    parts.append(lambda: exp(c - 2, m4, l2_ps, l2_ready, minus_one if in_sort(c) else bias2, e2,
                                             h2_ready, exp2_ready))
                if item_in(c - 3):
                    parts.append(lambda: squares(c - 3, m4))
                    if not in_sort(c):
                        parts.append(lambda: variance(c - 3, m4))
                run(parts, beside)

            act.wait_ge(biases_ready, 1)
            walk(act, step, finish=finish, sort_batch=sort_batch, sums=copy_sums,
                 middle=lambda: copy_sums(NE - 1, 0)[-1]())

        @block.vector
        def _(dve):
            chain = [0]

            def link(ins):
                chain[0] += 1
                ins.then_inc(dve_chain, 1)
                dve.wait_ge(dve_chain, chain[0])

            V = nc.vector

            def constants():
                dve.wait_ge(consts_made, 3)
                V.memset(zeros[:], 0.0)
                V.memset(minus_one[:], -1.0)
                V.memset(neg_half[:], -0.5)
                V.memset(eps[:], EPS)
                V.memset(ones[:], 1.0)
                V.memset(pay[:], 0.0)
                V.memset(pos[:], 0.0)
                V.memset(ones_f[:], 1.0)
                V.memset(ones_row[:], 1.0)
                V.memset(zeros_b[:], 0.0)
                V.memset(key[:], -1.0)
                V.tensor_copy(diff[:], diff_i[:])
                link(V.tensor_copy(count[:], count_i[:]))
                V.tensor_scalar(before[:], diff[:], 0.0, None, ALU.is_gt)
                V.tensor_scalar(not_before[:], diff[:], 0.0, None, ALU.is_le)
                V.tensor_scalar(next_row[:], diff[:], -1.0, None, ALU.is_equal)
                V.tensor_scalar(next_col[:], diff[:], float(EP - 1), None, ALU.is_equal)
                V.tensor_scalar(ident[:], diff[:], 0.0, None, ALU.is_equal)
                V.tensor_scalar(center[:], diff[:], 0.0, -1.0 / P, ALU.is_equal, ALU.add)
                V.tensor_copy(pay[0:EP, 2, 0:EC], prow_i[0:EP, 0:1].to_broadcast([EP, EC]))
                V.tensor_copy(pay[0:EP, 3, 0:EC], count_i[0:EP, 0:EC])
                V.tensor_scalar(prow_half_i[:, 0:1], prow_i[:], 4, None, ALU.logical_shift_right)
                V.tensor_scalar(prow_half_i[:, 1:2], prow_i[:], HALF - 1, None, ALU.bitwise_and)
                link(V.tensor_scalar(count_half_i[:], count_i[:], 4, None, ALU.logical_shift_right))
                V.tensor_copy(prow_half[:], prow_half_i[:])
                link(V.tensor_copy(count_half[:], count_half_i[:]))
                V.tensor_scalar(same_block[:], count_half[:, 0:P], prow_half[:, 0:1], None, ALU.is_equal)
                link(V.tensor_scalar(same_half[:], count_half[:], prow_half[:, 1:2], None, ALU.is_equal))

            def biases():
                dve.wait_ge(weights_loaded, 16 * 7)
                link(V.reduce_sum(w3_sum[:], w3[:], AX_X))
                link(V.tensor_scalar(w3_mean[:], w3_sum[:], 1.0 / P, None, ALU.mult))
                V.tensor_scalar(w3c[:], w3[:], w3_mean[:, 0:1], None, ALU.subtract).then_inc(b3_ready, 1)
                hot_nibbles(0, 0)
                hot_nibbles(0, 1)
                dve.wait_ge(setup_mm, 1)
                V.tensor_copy(bias_x[:], l2_ps[:, 0:1]).then_inc(b3_ready, 1)
                link(V.tensor_scalar(bias2[:], l1_ps[:, 0:1], b_in[:, 1:2], None, ALU.add))
                V.tensor_scalar(neg_bias2[:], bias2[:], -1.0, None, ALU.mult)
                dve.wait_ge(setup_mm, 2)
                link(V.tensor_tensor(bias1[:], b_in[:, 0:1], z_ps[0][:, 0:1], ALU.subtract))
                V.tensor_scalar(neg_bias1[:], bias1[:], -1.0, None, ALU.mult)
                V.tensor_scalar(bias_rest[:, 0:1], bias1[:], 1.0, None, ALU.add)
                link(V.tensor_scalar(bias_rest[:, 1:2], bias2[:], 1.0, None, ALU.add))
                for part in range(3):
                    link(V.tensor_copy(bias_low[:], bias_rest[:]))
                    link(V.tensor_copy(bias_parts[:, :, part], bias_low[:]))
                    if part < 2:
                        link(V.tensor_tensor(bias_rest[:], bias_rest[:], bias_parts[:, :, part], ALU.subtract))
                V.memset(picked[:], 0.0).then_inc(biases_ready, 1)
                hot_nibbles(1, 0)
                dve.wait_ge(setup_mm, 3)
                V.tensor_copy(bias_rows[0:3, 0, :], z_ps[0][0:3, 0:P])
                V.tensor_copy(bias_rows[0:3, 1, :], z_ps[1][0:3, 0:P]).then_inc(biases_ready, 1)

            def digits():
                dve.wait_ge(src_loaded, 16)
                V.tensor_scalar(digit_i[0:EP, 0, :], src_i[0:EP, :], 8, None, ALU.logical_shift_right)
                link(V.tensor_scalar(digit_i[0:EP, 1, :], src_i[0:EP, :], DIG - 1, None, ALU.bitwise_and))
                link(V.tensor_copy(pay[0:EP, 0:2, 0:EC], digit_i[0:EP, :, :]))

            def make_onehot(d, const, reg, slot):
                V.tensor_scalar(onehot[0:EP, slot, :], count[0:EP, :], cut(pay[0:EP, d, :], const, reg, 1), None,
                                ALU.is_equal).then_inc(onehot_ready, 1)

            def nibbles():
                for n in range(2):
                    V.tensor_scalar(nibble_i[0:EP, n, 0, :], digit_i[0:EP, 1 - n, :], 4, None, ALU.logical_shift_right)
                    last = V.tensor_scalar(nibble_i[0:EP, n, 1, :], digit_i[0:EP, 1 - n, :], HALF - 1, None, ALU.bitwise_and)
                link(last)
                link(V.tensor_copy(nibble[0:EP, :, :, :], nibble_i[0:EP, :, :, :]))
                dve.wait_ge(tables_cleared, 1)

            def hot_nibbles(n, k):
                V.tensor_tensor(nibble_hot[0:EP, n, k, 0:EC * HALF].rearrange("p (c v) -> p c v", v=HALF),
                                nibble[0:EP, n, k, :].rearrange("p (c a) -> p c a", a=1).to_broadcast([EP, EC, HALF]),
                                count[0:EP, 0:HALF].rearrange("p (a v) -> p a v", a=1).to_broadcast([EP, EC, HALF]),
                                ALU.is_equal).then_inc(nibbles_ready, 1)

            def hist(c):
                def fold():
                    for n in range(2):
                        dve.wait_ge(blocks_counted, n + 1)
                        last = V.tensor_tensor(block_sum[:, n, :], rank_ps[n][:, 0:P], same_block[:], ALU.mult)
                    link(last)
                    link(V.reduce_sum(half_sum[:], block_sum[:].rearrange("p n (k v) -> p n v k", v=HALF), AX_X))
                    for n in range(2):
                        V.tensor_tensor(digit_sum[:, n, :].rearrange("p (a v) -> p a v", v=HALF),
                                        half_sum[:, n, :].rearrange("p (a v) -> p a v", a=1).to_broadcast([P, HALF, HALF]),
                                        same_half[:].rearrange("p (a v) -> p a v", v=HALF), ALU.mult).then_inc(digits_folded, 1)

                return [fold if c == 0 else starts]

            def starts():
                dve.wait_ge(hist_done, 2)
                for n in range(2):
                    last = V.tensor_tensor_scan(totals[0:EP, n, :], rank_ps[n][0:EP, 0:DIG], zeros[0:EP, :], 0.0, ALU.add, ALU.add)
                link(last)
                for n in range(2):
                    last = V.tensor_tensor(start[0:EP, n, :], totals[0:EP, n, :], rank_ps[n][0:EP, 0:DIG], ALU.subtract)
                link(last)
                link(V.tensor_copy(start_i[0:EP, 0, :, :], start[0:EP, :, :]))
                V.tensor_scalar(start_i[0:EP, 1, :, :], start_i[0:EP, 0, :, :], 127, None, ALU.bitwise_and)
                link(V.tensor_scalar(start_i[0:EP, 2, :, :], start_i[0:EP, 0, :, :], 65536 - 128, None, ALU.bitwise_and))
                link(V.tensor_copy(start_b[0:EP, :, :, :], start_i[0:EP, 1:3, :, :]))
                dve.sem_inc(rank_free, 1)
                dve.sem_inc(start_ready, 1)

            def sort_batch(n, t, r):
                reg, r3 = times(r, UNIT), times(r, 3)
                ranked = n * (EC + 1)
                old = UNIT * (t - 2)
                known = 3 * (n * PASS + t - 2)

                def digit(u):
                    if not in_pass(t):
                        return
                    c = UNIT * t + u
                    at_least(dve, rank_ready, ranked + c - 6, reg)
                    make_onehot(1 - n, c, reg, c % (2 * UNIT))

                def extract(u):
                    if not in_pass(t - 1 if u >= 0 else t - 2):
                        return
                    c = UNIT * (t - 1) + u
                    at_least(dve, rank_ready, ranked + c + 2, reg)
                    V.scalar_tensor_tensor(out=picked[0:EP, c % 2, :], in0=rank_ps[c % 2][0:EP, 0:DIG], scalar=0.0,
                                           in1=onehot[0:EP, c % (2 * UNIT), :], op0=ALU.add, op1=ALU.mult,
                                           accum_out=cut(pos[0:EP, :], c, reg, 1)).then_inc(rank_free, 1)

                def quotient():
                    if not in_pass(t - 2):
                        return
                    at_least(dve, rank_free, n * EC + old + UNIT + 1, reg)
                    V.tensor_scalar(cut(quot[0:EP, :], old, reg, UNIT), cut(pos[0:EP, :], old, reg, UNIT),
                                    1.0 / EP, -(EP // 2) / EP, ALU.mult, ALU.add).then_inc(place_known, 1)

                def column():
                    if not in_pass(t - 2):
                        return
                    at_least(dve, place_known, known + 1, r3)
                    V.tensor_scalar(cut(pos_col[0:EP, :], old, reg, UNIT), cut(quot[0:EP, :], old, reg, UNIT),
                                    ROUND, ROUND, ALU.add, ALU.subtract).then_inc(place_known, 1)

                def row():
                    if not in_pass(t - 2):
                        return
                    at_least(dve, place_known, known + 2, r3)
                    V.scalar_tensor_tensor(out=cut(pos_row[0:EP, :], old, reg, UNIT), in0=cut(pos_col[0:EP, :], old, reg, UNIT),
                                           scalar=-float(EP), in1=cut(pos[0:EP, :], old, reg, UNIT),
                                           op0=ALU.mult, op1=ALU.add).then_inc(place_known, 1)

                def hots(u):
                    if not in_pass(t - 2):
                        return
                    if u == 0:
                        at_least(dve, place_known, known + 3, r3)
                    at_least(dve, place_free, n * EC + old + u - 2 * UNIT + 1, reg)
                    slot = UNIT * ((t - 2) % 4) + u
                    V.tensor_scalar(row_hot[0:EP, slot, :], count[0:EP, 0:EP], cut(pos_row[0:EP, :], old + u, reg, 1), None,
                                    ALU.is_equal)
                    V.tensor_scalar(col_hot[0:EP, slot, :], count[0:EP, 0:EC], cut(pos_col[0:EP, :], old + u, reg, 1), None,
                                    ALU.is_equal).then_inc(col_ready, 1)

                return [lambda: (extract(-1), digit(0), quotient(), digit(1), column()),
                        lambda: (extract(0), row(), digit(2), hots(0)),
                        lambda: (extract(1), hots(1)),
                        lambda: (extract(2), digit(3), hots(2)),
                        lambda: (extract(3), digit(4), hots(3), hots(4))]

            def finish(n):
                if n == 0:
                    dve.sem_inc(pay_ready, 1)
                else:
                    dve.wait_ge(permuted, n)
                    V.tensor_copy(pay[0:EP, :, 0:EC], perm_ps[0:EP, 0:NPAY * EC].rearrange("p (k c) -> p k c", k=NPAY))\
                        .then_inc(pay_ready, 1)
                dve.wait_ge(pay_ready, n + 1)

            def attr_indices(g, r):
                gp = g % SLOTS
                at_least(dve, attr_loaded[gp], 64 * (g // SLOTS), times(r, 64 // SLOTS))
                V.tensor_copy(attr_idx[0:EP, gp, :], cut(edge_i[0:EP, :], J * g, times(r, J), J)).then_inc(attr_idx_ready, 1)

            def x_indices(e, r):
                at_least(dve, x_gathered[e % SLOTS], 64 * (e // SLOTS), times(r, 64 // SLOTS))
                V.tensor_copy(x_idx[0:EP, e % SLOTS, :], cut(key_i[0:EP, :], J * e, times(r, J), J)).then_inc(x_idx_ready, 1)

            def next_indices(g, r):
                if 0 <= g < NE - SLOTS:
                    attr_indices(g + SLOTS, r)

            def carry_masks(e, r):
                at_least(dve, carry_mm, e, r)
                V.tensor_scalar(carry_mask[0:EC, e % 2, :], cut(keyB[0:EC, :], e * COLS, times(r, COLS), COLS),
                                keyT[0:EC, EP - 1:EP], None, ALU.is_equal).then_inc(carry_ready, 1)

            def add_carry(e, r):
                at_least(dve, carry_mm, e + 2, r)
                group = cut(sumT[:, :], e * COLS, times(r, COLS), COLS)
                V.tensor_tensor(group, rank_ps[e % 2][:, 0:COLS], group, ALU.add).then_inc(carried, 1)

            def gather(e, r):
                return [lambda: carry_masks(e + 1, r), list, list, lambda: add_carry(e, r)] + \
                    ([lambda: x_indices(e + 4, r)] if e + 4 < NE else [])

            def first():
                V.scalar_tensor_tensor(out=edge_f[0:EP, :], in0=pay[0:EP, 2, 0:EC], scalar=float(EC),
                                       in1=pay[0:EP, 3, 0:EC], op0=ALU.mult, op1=ALU.add)
                V.scalar_tensor_tensor(out=key[0:EP, 0:EC], in0=pay[0:EP, 0, 0:EC], scalar=float(DIG),
                                       in1=pay[0:EP, 1, 0:EC], op0=ALU.mult, op1=ALU.add).then_inc(key_ready, 1)
                dve.wait_ge(key_ready, 1)
                V.tensor_copy(key_i[0:EP, :], key[0:EP, 0:EC])
                V.tensor_copy(edge_i[0:EP, :], edge_f[0:EP, :])
                dve.wait_ge(key_mm, 2)
                V.tensor_copy(keyT[0:EC, :], perm_ps[0:EC, 0:EP]).then_inc(keyT_ready, 1)
                link(V.tensor_tensor(dup[0:EP, :], key[0:EP, 0:EC], rank_ps[0][0:EP, 0:EC], ALU.is_equal))
                link(V.scalar_tensor_tensor(out=target[0:EP, :], in0=dup[0:EP, :], scalar=SKIP, in1=key[0:EP, 0:EC],
                                            op0=ALU.mult, op1=ALU.add))
                V.tensor_copy(target_i[0:EP, :], target[0:EP, :]).then_inc(index_ready, 1)
                dve.wait_ge(index_ready, 1)
                for g in range(SLOTS):
                    attr_indices(g, 0)
                    x_indices(g, 0)

            def before_sums():
                dve.wait_ge(keyB_loaded, 16)
                for part in sums(-1, 0):
                    part()

            def sums(g, r):
                def one(j):
                    def do():
                        c = J * (g + 1) + j
                        if c == J * 2:
                            dve.wait_ge(keyB_loaded, 16 * KEY_PARTS)
                        at_least(dve, same_free, c + 1, times(r, J))
                        V.tensor_scalar(same[0:EP, c % (2 * J), :], cut(keyB[0:EP, :], EP * c, times(r, J * EP), EP),
                                        cut(key[0:EP, :], c, times(r, J), 1), None, ALU.is_equal).then_inc(same_ready, 1)
                    return do
                return [one(j) for j in range(J)] + [lambda: next_indices(g, r)]

            def middle():
                dve.wait_ge(sum_ready, NE + 2)
                last = sumT[:, :].rearrange("p (c e) -> p c e", e=EP)[:, :, EP - 1]
                V.tensor_copy(lastT[:], last).then_inc(last_ready, 1)
                dve.wait_ge(last_ready, 1)
                V.memset(last, 0.0)
                dve.wait_ge(last_turned, 1)
                V.tensor_copy(last_sum[0:EC, :], perm_ps[0:EC, 0:P]).then_inc(last_sum_ready, 1)
                carry_masks(0, 0)

            def elu(s, c, m4, ps, bias, neg_bias, e, exp_ready, mn, min_ready, h, used, done):
                n = cols(c)
                at_least(dve, exp_ready, c + 1, m4)
                if in_sort(s):
                    at_least(dve, used, c - 1, m4)
                    V.scalar_tensor_tensor(out=h[:, c % 2, 0:n], in0=e[:, c % 2, 0:n], scalar=1.0, in1=ps[:, 0:n],
                                           op0=ALU.min, op1=ALU.max).then_inc(done, 1)
                    return
                at_least(dve, done, c - 1, m4)
                V.tensor_scalar(mn[:, c % 2, 0:n], e[:, c % 2, 0:n], 1.0, bias[:, 0:1], ALU.min, ALU.add).then_inc(min_ready, 1)
                at_least(dve, min_ready, c + 1 - (items_in_sort(s - c) if s >= AT_KEYS else 0), m4)
                at_least(dve, used, c - 1, m4)
                V.scalar_tensor_tensor(out=h[:, c % 2, 0:n], in0=ps[:, 0:n], scalar=neg_bias[:, 0:1],
                                       in1=mn[:, c % 2, 0:n], op0=ALU.max, op1=ALU.add).then_inc(done, 1)

            def normalise(c, m4, m):
                k = c % SLOTS
                q = rows(c)
                at_least(dve, rstd_ready, c + 1, m4)
                if is_edge(c):
                    if c - SLOTS < ND:
                        dve.wait_ge(stored[k], 16 * DENSE_ON[k])
                    at_least(dve, scattered[k], 64 * ((c - ND) // SLOTS), times(m, 64))
                    V.tensor_copy(out_idx[0:EP, k, :], cut(target_i[0:EP, :], (c - ND) * J, times(m, 4 * J), J))
                else:
                    at_least(dve, stored[k], 16 * (c // SLOTS), times(m, 16))
                V.tensor_tensor(o_sb[q, k, :].rearrange("p (j f) -> p j f", j=J),
                                z_ps[c % 2][q, :].rearrange("p (j f) -> p j f", j=J),
                                rstd[q, c % 2, :].rearrange("p (j a) -> p j a", a=1).to_broadcast([q.stop, J, P]),
                                ALU.mult).then_inc(o_ready, 1)

            def step(c, m4, m, beside):
                def first_layer():
                    if item_in(c - 1):
                        elu(c, c - 1, m4, l1_ps, bias1, neg_bias1, e1, exp1_ready, m1, min1_ready, h1, l2_ready, h1_ready)

                def second_layer():
                    if item_in(c - 2):
                        elu(c, c - 2, m4, l2_ps, bias2, neg_bias2, e2, exp2_ready, m2, min2_ready, h2, z_ready, h2_ready)

                def output():
                    if item_in(c - 4):
                        normalise(c - 4, m4, m)

                parts = [list, first_layer, output, second_layer]
                if not in_sort(c):
                    parts = [list, first_layer, lambda: (output(), second_layer())]
                run(parts, beside)

            constants()
            digits()
            nibbles()
            biases()
            hot_nibbles(1, 1)
            walk(dve, step, hist=hist, sort_batch=sort_batch, finish=finish, first=first, before_sums=before_sums,
                 sums=sums, middle=middle, gather=gather, after_gather=lambda: add_carry(NE - 1, 0))


_INS = ['x', 'src', 'edge_attr_128', 'L0_gnn_W0', 'L0_gnn_b0', 'L0_gnn_W2', 'L0_gnn_b2', 'L0_gnn_W3', 'L0_gnn_b3']


def kernel(**inputs):
    import numpy as _np
    import concourse.bacc as _bacc
    from concourse import mybir as _mybir
    from concourse.bass_utils import run_bass_kernel_spmd as _run

    nc = _bacc.Bacc("TRN2", target_bir_lowering=False, num_devices=1)
    arrays, args = {}, []
    for name in _INS:
        a = _np.ascontiguousarray(inputs[name])
        arrays[f"in_{name}_dram"] = a
        args.append(nc.dram_tensor(f"in_{name}_dram", a.shape, _mybir.dt.from_np(a.dtype), kind="ExternalInput").ap())
    key_rows = nc.dram_tensor("key_rows_dram", inputs['src'].shape, _mybir.dt.float32, kind="Internal").ap()
    out = nc.dram_tensor("out_0_dram", inputs['x'].shape, _mybir.dt.float32, kind="ExternalOutput").ap()
    x_rows = nc.dram_tensor('x_rows_dram', (inputs['src'].shape[0] // J, J * inputs['x'].shape[1]), _mybir.dt.float32, kind='Internal').ap()
    gnn_resnorm(nc, *args, key_rows, x_rows, out)
    r = _run(nc, [arrays], core_ids=[0])
    return r.results[0]["out_0_dram"]
```
